# Optimizing a Trainium2 kernel written in Bass

```python
import numpy as np
import jax
import jax.numpy as jnp

def _softmax(x, axis=-1):
    return jax.nn.softmax(x, axis=axis)

def _gelu(x):
    return jax.nn.gelu(x, approximate=True)

def _silu(x):
    return jax.nn.silu(x)

def _sigmoid(x):
    return jax.nn.sigmoid(x)

def _layernorm(x, axis=-1, eps=1e-05):
    m = jnp.mean(x, axis=axis, keepdims=True)
    v = jnp.var(x, axis=axis, keepdims=True)
    return (x - m) / jnp.sqrt(v + eps)

def _scatter_add(tgt, idx, src, axis=0):
    return tgt.at[idx].add(src)

def _segment_sum(src, seg, n):
    return jax.ops.segment_sum(src, seg, n)
kernel_name = 'mk_cond_seq_d1_seqx_r4_6f64ac'

def setup_inputs(seed: int=0):
    np.random.seed(seed)
    _w = jnp.asarray

    def _rec_inputs():
        import jax
        import jax.numpy as jnp
        _rk = jax.random.key(seed)
        x = -7.109e-05 + 0.9999 * jax.random.normal(jax.random.fold_in(_rk, 1), (64, 64, 256), jnp.float32)
        _lenS = 64 - jax.random.randint(jax.random.fold_in(_rk, 7), (64,), 0, max(1, 64 // 4) + 1, jnp.int32)
        _lenS2 = 64 - jax.random.randint(jax.random.fold_in(_rk, 8), (64,), 0, max(1, 64 // 4) + 1, jnp.int32)
        itok_B_0_2 = jax.random.randint(jax.random.fold_in(_rk, 11), (64,), 0, 3, jnp.int32)
        return (x, itok_B_0_2)
    x, itok_B_0_2 = _rec_inputs()

    def _L0_cond_setup():
        import jax, jax.numpy as jnp
        import numpy as np
        H = 256
        EPS = 1e-05

        def _gelu(x):
            return jax.nn.gelu(x, approximate=False)
        key = jax.random.key(seed)
        ks = jax.random.split(key, 16)
        s = 1.0 / np.sqrt(H)
        inp = {'x': jax.random.normal(ks[0], (64, 256, H), dtype=jnp.float32), 'condition': jax.random.randint(ks[1], (64,), 0, 3), 'w1_nr': jax.random.normal(ks[2], (H, H), dtype=jnp.float32) * s, 'b1_nr': jnp.zeros((H,), dtype=jnp.float32), 'w2_nr': jax.random.normal(ks[3], (H, H), dtype=jnp.float32) * s, 'b2_nr': jnp.zeros((H,), dtype=jnp.float32), 'w1_tsr': jax.random.normal(ks[4], (H, H), dtype=jnp.float32) * s, 'b1_tsr': jnp.zeros((H,), dtype=jnp.float32), 'w2_tsr': jax.random.normal(ks[5], (H, H), dtype=jnp.float32) * s, 'b2_tsr': jnp.zeros((H,), dtype=jnp.float32), 'w1_sr': jax.random.normal(ks[6], (H, 2 * H), dtype=jnp.float32) * s, 'b1_sr': jnp.zeros((2 * H,), dtype=jnp.float32), 'w2_sr': jax.random.normal(ks[7], (2 * H, H), dtype=jnp.float32) * (1.0 / np.sqrt(2 * H)), 'b2_sr': jnp.zeros((H,), dtype=jnp.float32), 'w3_sr': jax.random.normal(ks[8], (H, H), dtype=jnp.float32) * s, 'b3_sr': jnp.zeros((H,), dtype=jnp.float32), 'gamma': jnp.ones((H,), dtype=jnp.float32), 'beta': jnp.zeros((H,), dtype=jnp.float32)}
        return inp
    _L0_cond_all = _L0_cond_setup()
    _L0_cond_in = {k: v for k, v in _L0_cond_all.items() if k in ('w1_nr', 'b1_nr', 'w2_nr', 'b2_nr', 'w1_tsr', 'b1_tsr', 'w2_tsr', 'b2_tsr', 'w1_sr', 'b1_sr', 'w2_sr', 'b2_sr', 'w3_sr', 'b3_sr', 'gamma', 'beta')}
    del _L0_cond_all
    return {'x': x, 'itok_B_0_2': itok_B_0_2, 'L0_cond_w1_nr': _L0_cond_in['w1_nr'], 'L0_cond_b1_nr': _L0_cond_in['b1_nr'], 'L0_cond_w2_nr': _L0_cond_in['w2_nr'], 'L0_cond_b2_nr': _L0_cond_in['b2_nr'], 'L0_cond_w1_tsr': _L0_cond_in['w1_tsr'], 'L0_cond_b1_tsr': _L0_cond_in['b1_tsr'], 'L0_cond_w2_tsr': _L0_cond_in['w2_tsr'], 'L0_cond_b2_tsr': _L0_cond_in['b2_tsr'], 'L0_cond_w1_sr': _L0_cond_in['w1_sr'], 'L0_cond_b1_sr': _L0_cond_in['b1_sr'], 'L0_cond_w2_sr': _L0_cond_in['w2_sr'], 'L0_cond_b2_sr': _L0_cond_in['b2_sr'], 'L0_cond_w3_sr': _L0_cond_in['w3_sr'], 'L0_cond_b3_sr': _L0_cond_in['b3_sr'], 'L0_cond_gamma': _L0_cond_in['gamma'], 'L0_cond_beta': _L0_cond_in['beta']}

def reference(x, itok_B_0_2, L0_cond_w1_nr, L0_cond_b1_nr, L0_cond_w2_nr, L0_cond_b2_nr, L0_cond_w1_tsr, L0_cond_b1_tsr, L0_cond_w2_tsr, L0_cond_b2_tsr, L0_cond_w1_sr, L0_cond_b1_sr, L0_cond_w2_sr, L0_cond_b2_sr, L0_cond_w3_sr, L0_cond_b3_sr, L0_cond_gamma, L0_cond_beta):
    import jax
    import jax.numpy as jnp

    def _L0_cond_ref(x, condition, w1_nr, b1_nr, w2_nr, b2_nr, w1_tsr, b1_tsr, w2_tsr, b2_tsr, w1_sr, b1_sr, w2_sr, b2_sr, w3_sr, b3_sr, gamma, beta):
        import jax, jax.numpy as jnp
        import numpy as np
        H = 256
        EPS = 1e-05

        def _gelu(x):
            return jax.nn.gelu(x, approximate=False)
        out_nr = _gelu(jnp.einsum('bth,hk->btk', x, w1_nr) + b1_nr)
        out_nr = jnp.einsum('bth,hk->btk', out_nr, w2_nr) + b2_nr
        out_tsr = _gelu(jnp.einsum('bth,hk->btk', x, w1_tsr) + b1_tsr)
        out_tsr = jnp.einsum('bth,hk->btk', out_tsr, w2_tsr) + b2_tsr
        h = _gelu(jnp.einsum('bth,hk->btk', x, w1_sr) + b1_sr)
        h = _gelu(jnp.einsum('bth,hk->btk', h, w2_sr) + b2_sr)
        out_sr = jnp.einsum('bth,hk->btk', h, w3_sr) + b3_sr
        c = condition[:, None, None]
        out = jnp.where(c == 0, out_nr, jnp.where(c == 1, out_tsr, jnp.where(c == 2, out_sr, jnp.zeros_like(x))))
        y = x + out
        mu = jnp.mean(y, axis=-1, keepdims=True)
        var = jnp.mean((y - mu) ** 2, axis=-1, keepdims=True)
        return (y - mu) * jax.lax.rsqrt(var + EPS) * gamma + beta
    x = _L0_cond_ref(x, itok_B_0_2, L0_cond_w1_nr, L0_cond_b1_nr, L0_cond_w2_nr, L0_cond_b2_nr, L0_cond_w1_tsr, L0_cond_b1_tsr, L0_cond_w2_tsr, L0_cond_b2_tsr, L0_cond_w1_sr, L0_cond_b1_sr, L0_cond_w2_sr, L0_cond_b2_sr, L0_cond_w3_sr, L0_cond_b3_sr, L0_cond_gamma, L0_cond_beta)
    return x

_drawn_inputs = setup_inputs


def setup_inputs(seed=0):
    import zlib

    import numpy as np

    out = dict(_drawn_inputs(seed))
    spreads = {'L0_cond_b1_nr': (0.0, 0.1),
     'L0_cond_b2_nr': (0.0, 0.1),
     'L0_cond_b1_tsr': (0.0, 0.1),
     'L0_cond_b2_tsr': (0.0, 0.1),
     'L0_cond_b1_sr': (0.0, 0.414),
     'L0_cond_b2_sr': (0.0, 0.279),
     'L0_cond_b3_sr': (0.0, 0.1),
     'L0_cond_gamma': (1.0, 0.2),
     'L0_cond_beta': (0.0, 0.1)}
    factors = {}
    for name, (base, spread) in spreads.items():
        noise = np.random.default_rng([zlib.crc32(name.encode()), seed]).standard_normal(out[name].shape)
        drawn = base * np.exp(spread * noise) if base else spread * noise
        out[name] = jnp.asarray(drawn.astype(out[name].dtype))
    for name, factor in factors.items():
        out[name] = (out[name] * factor).astype(out[name].dtype)
    return out
```

```python
from contextlib import ExitStack

import concourse.bass as bass
from concourse import mybir

ALU = mybir.AluOpType
ACT = mybir.ActivationFunctionType
AX = mybir.AxisListType
F32 = mybir.dt.float32
F32R = mybir.dt.float32r
I32 = mybir.dt.int32

P = 128
EPS = 1e-5
SR, NR, TSR, NONE, EMPTY = range(5)


def build_cond_mlp(nc, x, cond, w1_nr, b1_nr, w2_nr, b2_nr, w1_tsr, b1_tsr, w2_tsr, b2_tsr,
                   w1_sr, b1_sr, w2_sr, b2_sr, w3_sr, b3_sr, gamma, beta, out):
    B, T, H = x.shape
    KT = H // P
    HT = w1_sr.shape[1] // P
    PER = 512 // T
    TT = PER * T // P
    HALF = P // T
    ROUTES = 4
    SLOTS = B // PER + ROUTES - 1
    STEPS = SLOTS + 2
    PAIRS = (STEPS + 1) // 2
    PLACES = (2 * PAIRS + 4) * PER
    CLS = 2 * PAIRS + 4
    assert KT == 2 and HT == 4 and HALF == 2 and TT == 4

    with ExitStack() as ctx:
        def sb(name, shape, dt=F32):
            return ctx.enter_context(nc.sbuf_tensor(name, shape, dt))

        def sem(name):
            return ctx.enter_context(nc.semaphore(name))

        w1_raw = sb("w1_raw", [P, KT, 2 * 512])
        w1_hi = sb("w1_hi", [P, KT, 2 * 512], F32R)
        w1_lo = sb("w1_lo", [P, KT, 2 * 512], F32R)
        w2_raw = sb("w2_raw", [P, HT, H])
        w2_hi = sb("w2_hi", [P, HT, H], F32R)
        w2_lo = sb("w2_lo", [P, HT, H], F32R)
        wf_raw = sb("wf_raw", [P, ROUTES - 1, KT, H])
        wf_hi = sb("wf_hi", [P, ROUTES * KT * H], F32R)
        wf_lo = sb("wf_lo", [P, ROUTES * KT * H], F32R)
        bias_rows = sb("bias_rows", [16, P])
        bias_cols = sb("bias_cols", [P, 16])
        bf_all = sb("bf_all", [P, ROUTES * H])
        gamma_b = sb("gamma_b", [P, H])
        beta_b = sb("beta_b", [P, H])
        ident = sb("ident", [P, P])
        cond_b = sb("cond_b", [ROUTES, B], I32)
        cond_f = sb("cond_f", [ROUTES, B])
        key = sb("key", [ROUTES, 3, B])
        onehot = sb("onehot", [ROUTES, B])
        rank = sb("rank", [ROUTES, B])
        zeros = sb("zeros", [ROUTES, B])
        route_id = sb("route_id", [ROUTES, 1])
        full = sb("full", [ROUTES, B // PER])
        over = sb("over", [ROUTES, B // PER])
        groups = sb("groups", [ROUTES, 1])
        tri = sb("tri", [ROUTES, 2, ROUTES])
        bounds = sb("bounds", [ROUTES, 2])
        place_m = sb("place_m", [ROUTES, 2, B])
        ones4 = sb("ones4", [ROUTES, 1])
        step_id = sb("step_id", [ROUTES, CLS])
        ended = sb("ended", [ROUTES, 2, CLS])
        seq1 = sb("seq1", [B, 1])
        place_id = sb("place_id", [B, PLACES])
        place_col = sb("place_col", [B, 1])
        at_place = sb("at_place", [B, PLACES])
        cls_tab = sb("cls_tab", [1, CLS], I32)
        store_tab = sb("store_tab", [1, PLACES], I32)
        load_f = sb("load_f", [1, PLACES])
        load_tab = sb("load_tab", [1, PLACES], I32)
        x_in = [sb(f"x_in{p}", [P, TT, H]) for p in range(2)]
        x_hi = sb("x_hi", [P, KT, 512], F32R)
        x_lo = sb("x_lo", [P, KT, 512], F32R)
        a_act = sb("a_act", [P, 2, 512])
        b_act = sb("b_act", [P, 2, 512])
        c_act = sb("c_act", [P, 2, 512])
        h_hi = sb("h_hi", [P, HT, 512], F32R)
        h_lo = sb("h_lo", [P, HT, 512], F32R)
        f_hi = [sb(f"f_hi{p}", [P, KT, 512], F32R) for p in range(2)]
        f_lo = [sb(f"f_lo{p}", [P, KT, 512], F32R) for p in range(2)]
        y = [sb(f"y{p}", [P, TT, H]) for p in range(2)]
        stats = sb("stats", [P, TT, 6])
        diff, diff2, m2, mean_h = (sb(n, [P, TT]) for n in ("diff", "diff2", "m2", "mean_h"))
        neg_mean = [sb(f"neg_mean{p}", [P, TT]) for p in range(2)]
        hvar = [sb(f"hvar{p}", [P, TT]) for p in range(2)]
        half = sb("half", [P, TT])
        rstd = [sb(f"rstd{p}", [P, TT]) for p in range(2)]
        shift = [sb(f"shift{p}", [P, TT]) for p in range(2)]
        o = [sb(f"o{p}", [P, TT, H]) for p in range(2)]

        def bank(name):
            return ctx.enter_context(nc.psum_tensor(name, [P, 512], F32))

        ps_a = [bank(f"ps_a{m}") for m in range(2)]
        ps_b = [bank(f"ps_b{m}") for m in range(2)]
        ps_x = [bank(f"ps_x{m}") for m in range(KT)]
        ps_f = [bank(f"ps_f{m}") for m in range(2)]

        cond_in = sem("cond_in")
        w_in = [sem(f"w_in{i}") for i in range(7)]
        rows_in = sem("rows_in")
        bcast_in = sem("bcast_in")
        rows_zero = sem("rows_zero")
        consts = sem("consts")
        dve_step = sem("dve_step")
        w_hi_done = sem("w_hi_done")
        w_lo_done = sem("w_lo_done")
        rows_t = sem("rows_t")
        bias_done = sem("bias_done")
        groups_done = sem("groups_done")
        bounds_ps = sem("bounds_ps")
        place_done = sem("place_done")
        place_ps = sem("place_ps")
        onehot_done = sem("onehot_done")
        tabs_ps = sem("tabs_ps")
        tabs_done = sem("tabs_done")
        pool_step = sem("pool_step")
        x_loaded = [sem(f"x_loaded{p}") for p in range(2)]
        xT_ready = sem("xT_ready")
        x_hi_done = sem("x_hi_done")
        x_lo_done = sem("x_lo_done")
        a_ready, b_ready, c_ready = sem("a_ready"), sem("b_ready"), sem("c_ready")
        a_gelu, b_gelu, c_gelu = sem("a_gelu"), sem("b_gelu"), sem("c_gelu")
        a_split, b_split, c_split = sem("a_split"), sem("b_split"), sem("c_split")
        f_ready = sem("f_ready")
        xb_done = sem("xb_done")
        y_done = sem("y_done")
        bn_done = sem("bn_done")
        mv_done = sem("mv_done")
        rstd_done = sem("rstd_done")
        z_done = sem("z_done")
        gam_done = sem("gam_done")
        rstd_step = sem("rstd_step")
        agg_step = sem("agg_step")
        a_half, b_half, c_half = sem("a_half"), sem("b_half"), sem("c_half")
        o_done = sem("o_done")
        sp_turn = sem("sp_turn")
        stored = [sem(f"stored{p}") for p in range(2)]

        AHEAD = 2

        def upto(g, per=1, k=None):
            return (g + AHEAD) * per + (per if k is None else k + 1)


        W_PARTS = [
            (w1_raw[:, :, 0:512], w1_sr.rearrange("(k p) n -> p k n", p=P),
             w1_hi[:, :, 0:512], w1_lo[:, :, 0:512]),
            (w2_raw[:, :, :], w2_sr.rearrange("(k p) n -> p k n", p=P), w2_hi[:, :, :], w2_lo[:, :, :]),
            (w1_raw[:, :, 512:768], w1_nr.rearrange("(k p) n -> p k n", p=P),
             w1_hi[:, :, 512:768], w1_lo[:, :, 512:768]),
            (w1_raw[:, :, 768:1024], w1_tsr.rearrange("(k p) n -> p k n", p=P),
             w1_hi[:, :, 768:1024], w1_lo[:, :, 768:1024]),
        ]
        for r, w in ((SR, w3_sr), (NR, w2_nr), (TSR, w2_tsr)):
            cols = slice(r * KT * H, (r + 1) * KT * H)
            W_PARTS.append((wf_raw[:, r], w.rearrange("(k p) n -> p k n", p=P),
                            wf_hi[:, cols].rearrange("p (k n) -> p k n", k=KT),
                            wf_lo[:, cols].rearrange("p (k n) -> p k n", k=KT)))
        L1_COL = {SR: 0, NR: 512, TSR: 768}

        bounds_pt = ps_a[0][0:ROUTES, 0:2]
        place_pt = ps_a[1][0:B, 0:1]
        perm_pt = ps_f[0][0:1, 0:PLACES]
        cls_pt = ps_f[1][0:1, 0:CLS]
        bias_pt = ps_b[0][:, 0:16]

        block = ctx.enter_context(nc.Block())

        def register_set(eng, name, n):
            return [eng.alloc_register(f"{name}{j}") for j in range(n)]

        def load_values(eng, regs, table, at, hi):
            eng.load(regs, table[0:1, bass.ds(at, len(regs))])
            return [eng.snap(r, min_val=0, max_val=hi) for r in regs]

        @block.sync
        def _(sp):
            sp.dma_start(cond_b[:, :], cond.rearrange("(a b) -> a b", a=1).broadcast_to([ROUTES, B])
                         ).then_inc(cond_in, 16)
            for i, (raw, src, _, _) in enumerate(W_PARTS):
                sp.dma_start(raw, src).then_inc(w_in[i], 16)

            idx = register_set(sp, "sp_idx", PER)
            used = register_set(sp, "sp_used", PER)

            def load(g, p):
                for j, s in enumerate(load_values(sp, idx, load_tab, (g + 2) * PER, B - 1)):
                    row = (j % HALF) * T
                    sp.dma_start(x_in[p][row:row + T, j // HALF, :],
                                 x[bass.ds(s, 1), :, :].rearrange("a t h -> (a t) h")
                                 ).then_inc(x_loaded[p], 16)

            def store(g, p):
                sp.wait_ge(o_done, upto(g))
                sp.sem_inc(sp_turn, 1)
                taken = load_values(sp, used, store_tab, (g + 2) * PER, B)
                for j, s in enumerate(load_values(sp, idx, load_tab, (g + 2) * PER, B - 1)):
                    row = (j % HALF) * T
                    sp.dma_start(out[bass.ds(s, 1), :, :].rearrange("a t h -> (a t) h"),
                                 o[p][row:row + T, j // HALF, :], cond=(taken[j] > 0)
                                 ).then_inc(stored[p], 16)

            sp.wait_ge(tabs_done, 1)
            load(0, 0)
            load(1, 1)
            cls_regs = register_set(sp, "sp_cls", 6)
            with sp.Fori(0, PAIRS) as i:
                cls = load_values(sp, cls_regs, cls_tab, i * 2, EMPTY)
                for p in range(2):
                    g = i * 2 + p
                    with sp.If(cls[4 + p] < EMPTY):
                        sp.wait_ge(xT_ready, upto(g, KT))
                        sp.sem_inc(sp_turn, 1)
                        sp.wait_ge(xb_done, upto(g))
                        sp.sem_inc(sp_turn, 1)
                        load(g + 2, p)
                    with sp.If(cls[p] < EMPTY):
                        store(g - 2, p)
                    with sp.Else():
                        sp.sem_inc(stored[p], 16 * PER)
            for p in range(2):
                sp.wait_ge(stored[p], 16 * PER * PAIRS)

        @block.gpsimd
        def _(pool):
            nc.gpsimd.memset(ident[:, :], 0.0).then_inc(pool_step, 1)
            nc.gpsimd.memset(tri[:, :, :], 1.0).then_inc(pool_step, 1)
            nc.gpsimd.memset(bias_rows[:, :], 0.0).then_inc(pool_step, 1)
            nc.gpsimd.iota(route_id[:, :], [[0, 1]], base=0, channel_multiplier=1,
                           allow_small_or_imprecise_dtypes=True).then_inc(consts, 1)
            nc.gpsimd.iota(full[:, :], [[PER, B // PER]], base=0, channel_multiplier=0,
                           allow_small_or_imprecise_dtypes=True).then_inc(consts, 1)
            nc.gpsimd.iota(step_id[:, :], [[1, CLS]], base=-2, channel_multiplier=0,
                           allow_small_or_imprecise_dtypes=True).then_inc(consts, 1)
            nc.gpsimd.iota(seq1[:, :], [[0, 1]], base=1, channel_multiplier=1,
                           allow_small_or_imprecise_dtypes=True).then_inc(consts, 1)
            nc.gpsimd.iota(place_id[:, :], [[1, PLACES]], base=-2 * PER, channel_multiplier=0,
                           allow_small_or_imprecise_dtypes=True).then_inc(consts, 1)
            pool.wait_ge(pool_step, 3)
            for e in range(2):
                nc.gpsimd.affine_select(out=tri[:, e, :], in_=tri[:, e, :], compare_op=ALU.is_ge, fill=0.0,
                                        base=e - 1, pattern=[[1, ROUTES]], channel_multiplier=-1
                                        ).then_inc(consts, 1)
            nc.gpsimd.affine_select(out=ident[:, :], in_=ident[:, :], compare_op=ALU.not_equal, fill=1.0,
                                    base=0, pattern=[[-1, P]], channel_multiplier=1).then_inc(consts, 1)
            nc.gpsimd.memset(half[:, :], -0.5).then_inc(pool_step, 1)
            nc.gpsimd.memset(bf_all[:, NONE * H:(NONE + 1) * H], 0.0).then_inc(pool_step, 1)
            pool.wait_ge(pool_step, 5)
            pool.wait_ge(bcast_in, 16 * 5)
            nc.gpsimd.tensor_scalar(gamma_b[:, :], gamma_b[:, :], float(H) ** 0.5, None, ALU.mult
                                    ).then_inc(pool_step, 1)
            pool.wait_ge(pool_step, 6)

            for done, per in ((xb_done, 1), (gam_done, 1), (o_done, 1), (rstd_step, 1), (rstd_done, 1)):
                pool.sem_inc(done, AHEAD * per)
            cls_regs = register_set(pool, "pool_cls", 5)
            pool.wait_ge(tabs_done, 1)
            with pool.Fori(0, PAIRS) as i:
                cls = load_values(pool, cls_regs, cls_tab, i * 2, EMPTY)
                for p in range(2):
                    g = i * 2 + p
                    with pool.If(cls[2 + p] < EMPTY):
                        pool.wait_ge(x_loaded[p], 16 * PER * i + 16 * PER)
                        pool.wait_ge(z_done, upto(g - 2))
                        bias = bf_all[:, bass.ds(cls[2 + p].with_bounds(max_val=NONE) * H, H)]
                        nc.gpsimd.tensor_tensor(
                            y[p][:, :, :], x_in[p][:, :, :],
                            bias.rearrange("p (a h) -> p a h", a=1).broadcast_to([P, TT, H]),
                            ALU.add).then_inc(xb_done, 1)
                    with pool.If(cls[p] < EMPTY):
                        pool.wait_ge(z_done, upto(g - 2))
                        for src, done in ((gamma_b, gam_done), (beta_b, o_done)):
                            if done is o_done:
                                pool.wait_ge(gam_done, upto(g - 2))
                            nc.gpsimd.tensor_tensor(
                                o[p][:, :, :], o[p][:, :, :],
                                src[:, :].rearrange("p (a h) -> p a h", a=1).broadcast_to([P, TT, H]),
                                ALU.mult if done is gam_done else ALU.add).then_inc(done, 1)
                    with pool.If(cls[1 + p] < EMPTY):
                        q = 1 - p
                        pool.wait_ge(mv_done, upto(g - 1))
                        nc.gpsimd.tensor_tensor(rstd[q][:, :], hvar[q][:, :], half[:, :], ALU.pow
                                                ).then_inc(rstd_step, 1)
                        pool.wait_ge(rstd_step, upto(g - 1))
                        nc.gpsimd.tensor_tensor(shift[q][:, :], rstd[q][:, :], neg_mean[q][:, :], ALU.mult
                                                ).then_inc(rstd_done, 1)

        @block.scalar
        def _(act):
            act.wait_ge(pool_step, 3)
            for row, b in ((0, b1_sr), (4 * NR, b1_nr), (4 * TSR, b1_tsr), (14, b2_sr)):
                n = b.shape[0] // P
                act.dma_start(bias_rows[row:row + n, :], b.rearrange("(m p) -> m p", p=P)).then_inc(rows_in, 16)
            for dst, b in ((bf_all[:, SR * H:(SR + 1) * H], b3_sr), (bf_all[:, NR * H:(NR + 1) * H], b2_nr),
                           (bf_all[:, TSR * H:(TSR + 1) * H], b2_tsr), (gamma_b[:, :], gamma),
                           (beta_b[:, :], beta)):
                act.dma_start(dst, b.rearrange("(a n) -> a n", a=1).broadcast_to([P, H])).then_inc(bcast_in, 16)
            for i, (raw, _, hi, _) in enumerate(W_PARTS):
                act.wait_ge(w_in[i], 16)
                nc.scalar.activation(hi, raw, ACT.Copy).then_inc(w_hi_done, 1)
            for done, per in ((x_hi_done, KT), (a_gelu, 2), (b_gelu, 2), (c_gelu, 2), (z_done, 1)):
                act.sem_inc(done, AHEAD * per)
            act.wait_ge(bias_done, 1)

            def x_high(g):
                for kt in range(KT):
                    act.wait_ge(xT_ready, upto(g, KT, kt))
                    nc.scalar.activation(x_hi[:, kt, :], ps_x[kt][:, :], ACT.Copy).then_inc(x_hi_done, 1)

            x_high(0)
            cls_regs = register_set(act, "act_cls", 5)
            act.wait_ge(tabs_done, 1)
            with act.Fori(0, PAIRS) as i:
                cls = load_values(act, cls_regs, cls_tab, i * 2, EMPTY)
                for p in range(2):
                    g = i * 2 + p
                    with act.If(cls[2 + p] < EMPTY):
                        bias_at = act.snap(cls[2 + p].with_bounds(max_val=NONE) * 4)
                        for m in range(2):
                            act.wait_ge(a_ready, upto(g, 2, m))
                            act.wait_ge(a_split, upto(g - 1, 2, m))
                            nc.scalar.activation(a_act[:, m, :], ps_a[m][:, :], ACT.Gelu,
                                                 bias=bias_cols[:, bass.ds(bias_at + m, 1)]).then_inc(a_gelu, 1)
                    with act.If(cls[2 + p] < NR):
                        for m in range(2):
                            act.wait_ge(b_ready, upto(g, 2, m))
                            nc.scalar.activation(b_act[:, m, :], ps_b[m][:, :], ACT.Gelu,
                                                 bias=bias_cols[:, 2 + m:3 + m]).then_inc(b_gelu, 1)
                    with act.If(cls[3 + p] < EMPTY):
                        x_high(g + 1)
                    with act.If(cls[p] < EMPTY):
                        act.wait_ge(rstd_done, upto(g - 2))
                        act.wait_ge(stored[p], 16 * PER * i)
                        for t in range(TT):
                            z = nc.scalar.activation(o[p][:, t, :], y[p][:, t, :], ACT.Identity,
                                                     bias=shift[p][:, t:t + 1], scale=rstd[p][:, t:t + 1])
                        z.then_inc(z_done, 1)
                    with act.If(cls[2 + p] < NR):
                        for m in range(2):
                            act.wait_ge(c_ready, upto(g, 2, m))
                            nc.scalar.activation(c_act[:, m, :], ps_b[m][:, :], ACT.Gelu,
                                                 bias=bias_cols[:, 14 + m:15 + m]).then_inc(c_gelu, 1)

        @block.vector
        def _(dve):
            step = [0]

            def chain(ins):
                step[0] += 1
                ins.then_inc(dve_step, 1)
                dve.wait_ge(dve_step, step[0])

            chain(nc.vector.memset(ones4[:, :], 1.0))
            chain(nc.vector.memset(zeros[:, :], 0.0))
            dve.wait_ge(cond_in, 16)
            chain(nc.vector.tensor_copy(cond_f[:, :], cond_b[:, :]))
            for j, (value, less) in enumerate(((2, NONE - SR), (0, NONE - NR), (1, NONE - TSR))):
                chain(nc.vector.tensor_scalar(key[:, j, :], cond_f[:, :], float(value), float(-less),
                                              ALU.is_equal, ALU.mult))
            chain(nc.vector.tensor_tensor(key[:, 0, :], key[:, 0, :], key[:, 1, :], ALU.add))
            chain(nc.vector.scalar_tensor_tensor(out=key[:, 1, :], in0=key[:, 0, :], scalar=float(NONE),
                                                 in1=key[:, 2, :], op0=ALU.add, op1=ALU.add))
            dve.wait_ge(consts, 8)
            chain(nc.vector.tensor_scalar(onehot[:, :], key[:, 1, :], route_id[:, 0:1], None, ALU.is_equal))
            chain(nc.vector.tensor_tensor_scan(rank[:, :], onehot[:, :], zeros[:, :], 0.0, ALU.add, ALU.add))
            chain(nc.vector.tensor_scalar(over[:, :], full[:, :], rank[:, B - 1:B], None, ALU.is_lt))
            nc.vector.tensor_reduce(groups[:, :], over[:, :], AX.X, ALU.add).then_inc(groups_done, 1)
            dve.wait_ge(bounds_ps, 1)
            chain(nc.vector.tensor_copy(bounds[:, :], bounds_pt))
            chain(nc.vector.tensor_scalar(place_m[:, 0, :], rank[:, :], -1.0, None, ALU.add))
            chain(nc.vector.tensor_scalar(bounds[:, 0:1], bounds[:, 0:1], float(PER), None, ALU.mult))
            chain(nc.vector.tensor_scalar(place_m[:, 0, :], place_m[:, 0, :], bounds[:, 0:1], None, ALU.add))
            nc.vector.tensor_tensor(place_m[:, 1, :], place_m[:, 0, :], onehot[:, :], ALU.mult
                                    ).then_inc(place_done, 1)
            chain(nc.vector.tensor_scalar(ended[:, 0, :], step_id[:, :], bounds[:, 1:2], None, ALU.is_ge))
            chain(nc.vector.tensor_scalar(ended[:, 1, :], step_id[:, :], 0.0, None, ALU.is_lt))
            chain(nc.vector.tensor_tensor(ended[:, 0, :], ended[:, 0, :], ended[:, 1, :], ALU.add))
            dve.wait_ge(place_ps, 1)
            chain(nc.vector.tensor_copy(place_col[:, :], place_pt))
            nc.vector.tensor_scalar(at_place[:, :], place_id[:, :], place_col[:, 0:1], None, ALU.is_equal
                                    ).then_inc(onehot_done, 1)
            dve.wait_ge(tabs_ps, 1)
            nc.vector.tensor_copy(cls_tab[:, :], cls_pt)
            nc.vector.tensor_copy(store_tab[:, :], perm_pt)
            chain(nc.vector.tensor_scalar(load_f[:, :], perm_pt, -1.0, 0.0, ALU.add, ALU.max))
            nc.vector.tensor_copy(load_tab[:, :], load_f[:, :]).then_inc(tabs_done, 1)

            dve.wait_ge(rows_t, 1)
            nc.vector.tensor_copy(bias_cols[:, :], bias_pt).then_inc(bias_done, 1)
            for w in (wf_hi, wf_lo):
                nc.vector.memset(w[:, NONE * KT * H:(NONE + 1) * KT * H].bitcast(F32), 0.0)
            for i, (raw, _, hi, lo) in enumerate(W_PARTS):
                dve.wait_ge(w_hi_done, i + 1)
                nc.vector.tensor_tensor(lo, raw, hi.bitcast(F32), ALU.subtract).then_inc(w_lo_done, 1)
            for done, per in ((x_lo_done, KT), (a_half, 2), (a_split, 2), (b_half, 2), (b_split, 2), (c_half, 2),
                              (c_split, 2), (y_done, 2), (bn_done, TT), (agg_step, 4), (mv_done, 1)):
                dve.sem_inc(done, AHEAD * per)

            def x_low(g):
                for kt in range(KT):
                    dve.wait_ge(x_hi_done, upto(g, KT, kt))
                    nc.vector.tensor_tensor(x_lo[:, kt, :], ps_x[kt][:, :], x_hi[:, kt, :].bitcast(F32),
                                            ALU.subtract).then_inc(x_lo_done, 1)

            def split(src, hi, lo, half_done, hi_count, done):
                nc.vector.tensor_copy(hi, src).then_inc(half_done, 1)
                dve.wait_ge(half_done, hi_count)
                nc.vector.tensor_tensor(lo, src, hi.bitcast(F32), ALU.subtract).then_inc(done, 1)

            x_low(0)
            cls_regs = register_set(dve, "dve_cls", 5)
            with dve.Fori(0, PAIRS) as i:
                cls = load_values(dve, cls_regs, cls_tab, i * 2, EMPTY)
                for p in range(2):
                    g = i * 2 + p
                    with dve.If(cls[2 + p] < NR):
                        for m in range(2):
                            dve.wait_ge(a_gelu, upto(g, 2, m))
                            split(a_act[:, m, :], h_hi[:, m, :], h_lo[:, m, :], a_half, upto(g, 2, m), a_split)
                        for m in range(2):
                            dve.wait_ge(b_gelu, upto(g, 2, m))
                            split(b_act[:, m, :], h_hi[:, 2 + m, :], h_lo[:, 2 + m, :],
                                  b_half, upto(g, 2, m), b_split)
                    with dve.Else():
                        with dve.If(cls[2 + p] < EMPTY):
                            for m in range(2):
                                dve.wait_ge(a_gelu, upto(g, 2, m))
                                split(a_act[:, m, :], f_hi[p][:, m, :], f_lo[p][:, m, :],
                                      a_half, upto(g, 2, m), a_split)
                    with dve.If(cls[3 + p] < EMPTY):
                        x_low(g + 1)
                    with dve.If(cls[1 + p] < EMPTY):
                        q = 1 - p
                        dve.wait_ge(xb_done, upto(g - 1))
                        for b in range(2):
                            dve.wait_ge(f_ready, upto(g - 1, 2, b))
                            nc.vector.tensor_tensor(
                                y[q][:, 2 * b:2 * b + 2, :], ps_f[b][:, :].rearrange("p (t h) -> p t h", t=2),
                                y[q][:, 2 * b:2 * b + 2, :], ALU.add).then_inc(y_done, 1)
                        for t in range(TT):
                            dve.wait_ge(y_done, upto(g - 1, 2, t // 2))
                            nc.vector.bn_stats(stats[:, t, :], y[q][:, t, :]).then_inc(bn_done, 1)
                        mean_e, m2_e, mean_o, m2_o = (stats[:, :, c] for c in (1, 2, 4, 5))
                        dve.wait_ge(bn_done, upto(g - 1, TT))
                        nc.vector.tensor_tensor(diff[:, :], mean_e, mean_o, ALU.subtract).then_inc(agg_step, 1)
                        nc.vector.tensor_tensor(m2[:, :], m2_e, m2_o, ALU.add).then_inc(agg_step, 1)
                        nc.vector.tensor_scalar(mean_h[:, :], mean_e, -0.5, None, ALU.mult).then_inc(agg_step, 1)
                        dve.wait_ge(agg_step, upto(g - 1, 4, 0))
                        nc.vector.scalar_tensor_tensor(out=diff2[:, :], in0=diff[:, :], scalar=H / 4.0,
                                                       in1=diff[:, :], op0=ALU.mult, op1=ALU.mult
                                                       ).then_inc(agg_step, 1)
                        dve.wait_ge(agg_step, upto(g - 1, 4, 2))
                        nc.vector.scalar_tensor_tensor(out=neg_mean[q][:, :], in0=mean_o, scalar=-0.5,
                                                       in1=mean_h[:, :], op0=ALU.mult, op1=ALU.add)
                        dve.wait_ge(agg_step, upto(g - 1, 4, 3))
                        nc.vector.scalar_tensor_tensor(out=hvar[q][:, :], in0=m2[:, :], scalar=H * EPS,
                                                       in1=diff2[:, :], op0=ALU.add, op1=ALU.add
                                                       ).then_inc(mv_done, 1)
                    with dve.If(cls[2 + p] < NR):
                        for m in range(2):
                            dve.wait_ge(c_gelu, upto(g, 2, m))
                            split(c_act[:, m, :], f_hi[p][:, m, :], f_lo[p][:, m, :],
                                  c_half, upto(g, 2, m), c_split)

        @block.tensor
        def _(pe):
            pe.wait_ge(consts, 8)
            pe.wait_ge(groups_done, 1)
            for e in range(2):
                mm = nc.tensor.matmul(bounds_pt[:, e:e + 1], tri[:, e, :], groups[:, :], start=True, stop=True)
            mm.then_inc(bounds_ps, 1)
            pe.wait_ge(place_done, 1)
            nc.tensor.matmul(place_pt, place_m[:, 1, :], ones4[:, :], start=True, stop=True).then_inc(place_ps, 1)
            pe.wait_ge(onehot_done, 1)
            nc.tensor.matmul(perm_pt, seq1[:, :], at_place[:, :], start=True, stop=True)
            nc.tensor.matmul(cls_pt, ones4[:, :], ended[:, 0, :], start=True, stop=True).then_inc(tabs_ps, 1)
            pe.wait_ge(rows_in, 16 * 4)
            nc.tensor.transpose(bias_pt, bias_rows[:, :], ident[0:16, 0:16]).then_inc(rows_t, 1)

            def transpose_x(g, p, nth):
                pe.wait_ge(x_loaded[p], 16 * PER * nth)
                for kt in range(KT):
                    for t in range(TT):
                        mm = nc.tensor.transpose(ps_x[kt][:, t * P:(t + 1) * P],
                                                 x_in[p][:, t, kt * P:(kt + 1) * P], ident[:, :])
                    mm.then_inc(xT_ready, 1)

            def layer1(route, m, dst):
                cols = slice(L1_COL[route] + m * P, L1_COL[route] + (m + 1) * P)
                for kt in range(KT):
                    nc.tensor.matmul(dst, w1_lo[:, kt, cols], x_hi[:, kt, :], start=(kt == 0), stop=False)
                    nc.tensor.matmul(dst, w1_hi[:, kt, cols], x_lo[:, kt, :], start=False, stop=False)
                    mm = nc.tensor.matmul(dst, w1_hi[:, kt, cols], x_hi[:, kt, :], start=False,
                                          stop=(kt == KT - 1))
                return mm

            def layer1_a(route, g):
                for m in range(2):
                    pe.wait_ge(a_gelu, upto(g - 1, 2, m))
                    layer1(route, m, ps_a[m][:, :]).then_inc(a_ready, 1)

            for done, per in ((xT_ready, KT), (a_ready, 2), (b_ready, 2), (c_ready, 2), (f_ready, 2)):
                pe.sem_inc(done, AHEAD * per)
            pe.wait_ge(bias_done, 1)
            pe.wait_ge(tabs_done, 1)
            transpose_x(0, 0, 1)
            pe.wait_ge(w_lo_done, len(W_PARTS))
            cls_regs = register_set(pe, "pe_cls", 5)
            with pe.Fori(0, PAIRS) as i:
                cls = load_values(pe, cls_regs, cls_tab, i * 2, EMPTY)
                for p in range(2):
                    g = i * 2 + p
                    with pe.If(cls[2 + p] < EMPTY):
                        pe.wait_ge(x_lo_done, upto(g, KT))
                    with pe.If(cls[2 + p] < NR):
                        layer1_a(SR, g)
                        for m in range(2):
                            if m == 0:
                                pe.wait_ge(c_gelu, upto(g - 1, 2))
                            layer1(SR, 2 + m, ps_b[m][:, :]).then_inc(b_ready, 1)
                    with pe.Else():
                        with pe.If(cls[2 + p] < TSR):
                            layer1_a(NR, g)
                        with pe.Else():
                            with pe.If(cls[2 + p] < EMPTY):
                                layer1_a(TSR, g)
                    with pe.If(cls[3 + p] < EMPTY):
                        transpose_x(g + 1, 1 - p, i + 1 + p)
                    with pe.If(cls[1 + p] < EMPTY):
                        q = 1 - p
                        pe.wait_ge(a_split, upto(g - 1, 2))
                        with pe.If(cls[1 + p] < NR):
                            pe.wait_ge(c_split, upto(g - 1, 2))
                        f_at = pe.snap(cls[1 + p].with_bounds(max_val=NONE) * (KT * H))
                        for t in range(TT):
                            dst = ps_f[t // 2][:, (t % 2) * H:(t % 2 + 1) * H]
                            if t % 2 == 0:
                                pe.wait_ge(y_done, upto(g - 2, 2, t // 2))
                            for kt in range(KT):
                                toks = slice(t * P, (t + 1) * P)
                                w_hi = wf_hi[:, bass.ds(f_at + kt * H, H)]
                                w_lo = wf_lo[:, bass.ds(f_at + kt * H, H)]
                                nc.tensor.matmul(dst, f_lo[q][:, kt, toks], w_hi, start=(kt == 0), stop=False)
                                nc.tensor.matmul(dst, f_hi[q][:, kt, toks], w_lo, start=False, stop=False)
                                mm = nc.tensor.matmul(dst, f_hi[q][:, kt, toks], w_hi, start=False,
                                                      stop=(kt == KT - 1))
                            if t % 2:
                                mm.then_inc(f_ready, 1)
                    with pe.If(cls[2 + p] < NR):
                        for m in range(2):
                            dst = ps_b[m][:, :]
                            cols = slice(m * P, (m + 1) * P)
                            pe.wait_ge(b_gelu, upto(g, 2, m))
                            for kt in range(HT):
                                if m == 0 and kt == 0:
                                    pe.wait_ge(a_split, upto(g, 2))
                                if m == 0 and kt >= 2:
                                    pe.wait_ge(b_split, upto(g, 2, kt - 2))
                                nc.tensor.matmul(dst, w2_lo[:, kt, cols], h_hi[:, kt, :], start=(kt == 0),
                                                 stop=False)
                                nc.tensor.matmul(dst, w2_hi[:, kt, cols], h_lo[:, kt, :], start=False,
                                                 stop=False)
                                mm = nc.tensor.matmul(dst, w2_hi[:, kt, cols], h_hi[:, kt, :], start=False,
                                                      stop=(kt == HT - 1))
                            mm.then_inc(c_ready, 1)


INPUTS = ["x", "itok_B_0_2"] + ["L0_cond_" + n for n in (
    "w1_nr", "b1_nr", "w2_nr", "b2_nr", "w1_tsr", "b1_tsr", "w2_tsr", "b2_tsr",
    "w1_sr", "b1_sr", "w2_sr", "b2_sr", "w3_sr", "b3_sr", "gamma", "beta")]


def kernel(**inputs):
    import numpy as np
    import concourse.bacc as bacc
    from concourse.bass_utils import run_bass_kernel_spmd

    nc = bacc.Bacc("TRN2", target_bir_lowering=False, num_devices=1)
    arrays, args = {}, []
    for name in INPUTS:
        a = np.ascontiguousarray(inputs[name])
        arrays[f"{name}_dram"] = a
        args.append(nc.dram_tensor(f"{name}_dram", a.shape, mybir.dt.from_np(a.dtype), kind="ExternalInput").ap())
    args.append(nc.dram_tensor("out_dram", inputs["x"].shape, F32, kind="ExternalOutput").ap())
    build_cond_mlp(nc, *args)
    result = run_bass_kernel_spmd(nc, [arrays], core_ids=[0])
    return result.results[0]["out_dram"]
```

```python
from contextlib import ExitStack

import concourse.bass as bass
from concourse import mybir

ALU = mybir.AluOpType
ACT = mybir.ActivationFunctionType
AX = mybir.AxisListType
F32 = mybir.dt.float32
F32R = mybir.dt.float32r
I32 = mybir.dt.int32

P = 128
EPS = 1e-5
SR, NR, TSR, NONE, EMPTY = range(5)


def build_cond_mlp(nc, x, cond, w1_nr, b1_nr, w2_nr, b2_nr, w1_tsr, b1_tsr, w2_tsr, b2_tsr,
                   w1_sr, b1_sr, w2_sr, b2_sr, w3_sr, b3_sr, gamma, beta, out):
    B, T, H = x.shape
    KT = H // P
    HT = w1_sr.shape[1] // P
    PER = 512 // T
    TT = PER * T // P
    ROWS = P // PER
    ROUTES = 4
    SLOTS = B // PER + ROUTES - 1
    STEPS = SLOTS + 2
    RING = 4
    ROUNDS = -(-STEPS // RING)
    WINDOW = RING + 5
    CLS = RING * ROUNDS + 5
    PLACES = CLS * PER
    assert KT == 2 and HT == 4 and TT * ROWS == T and TT == 4

    with ExitStack() as ctx:
        def sb(name, shape, dt=F32):
            return ctx.enter_context(nc.sbuf_tensor(name, shape, dt))

        def sem(name):
            return ctx.enter_context(nc.semaphore(name))

        w1_raw = sb("w1_raw", [P, KT, 2 * 512])
        w1_hi = sb("w1_hi", [P, KT, 2 * 512], F32R)
        w1_lo = sb("w1_lo", [P, KT, 2 * 512], F32R)
        w2_raw = sb("w2_raw", [P, HT, H])
        w2_hi = sb("w2_hi", [P, HT, H], F32R)
        w2_lo = sb("w2_lo", [P, HT, H], F32R)
        wf_raw = sb("wf_raw", [P, ROUTES - 1, KT, H])
        wf_hi = sb("wf_hi", [P, ROUTES * KT * H], F32R)
        wf_lo = sb("wf_lo", [P, ROUTES * KT * H], F32R)
        bias_rows = sb("bias_rows", [16, P])
        bias_cols = sb("bias_cols", [P, 16])
        bf_raw = sb("bf_raw", [2, ROUTES * H])
        bf_round = sb("bf_round", [2, ROUTES * H], F32R)
        bf_parts = sb("bf_parts", [2, ROUTES * H], F32R)
        minus_row = sb("minus_row", [2, 1])
        ones2 = sb("ones2", [2, P], F32R)
        gamma_b = sb("gamma_b", [P, H])
        beta_b = sb("beta_b", [P, H])
        ident = sb("ident", [P, P])
        warm = sb("warm", [1, 1])
        cond_b = sb("cond_b", [ROUTES, B], I32)
        cond_f = sb("cond_f", [ROUTES, B])
        key = sb("key", [ROUTES, 3, B])
        onehot = sb("onehot", [ROUTES, B])
        rank = sb("rank", [ROUTES, B])
        zeros = sb("zeros", [ROUTES, B])
        route_id = sb("route_id", [ROUTES, 1])
        full = sb("full", [ROUTES, B // PER])
        over = sb("over", [ROUTES, B // PER])
        groups = sb("groups", [ROUTES, 1])
        tri = sb("tri", [ROUTES, 2, ROUTES])
        bounds = sb("bounds", [ROUTES, 2])
        place_m = sb("place_m", [ROUTES, 2, B])
        ones4 = sb("ones4", [ROUTES, 1])
        step_id = sb("step_id", [ROUTES, CLS])
        ended = sb("ended", [ROUTES, 2, CLS])
        seq1 = sb("seq1", [B, 1])
        place_id = sb("place_id", [B, PLACES])
        place_col = sb("place_col", [B, 1])
        at_place = sb("at_place", [B, PLACES])
        first_place = sb("first_place", [B, CLS + 1])
        reached = sb("reached", [B, CLS + 1])
        in_group = sb("in_group", [B, CLS])
        nth_group = sb("nth_group", [B, 1])
        in_place = sb("in_place", [B, 1])
        row_place = sb("row_place", [B, P])
        row_1 = sb("row_1", [B, P])
        row_at = sb("row_at", [B, P])
        row_f = sb("row_f", [P, CLS])
        row_idx = sb("row_idx", [P, CLS], I32)
        row_cur = sb("row_cur", [P, RING], I32)
        cls_tab = sb("cls_tab", [1, CLS], I32)
        store_tab = sb("store_tab", [1, PLACES], I32)
        load_f = sb("load_f", [1, PLACES])
        load_tab = sb("load_tab", [1, PLACES], I32)
        x_in = [sb(f"x_in{p}", [P, TT, H]) for p in range(RING)]
        x_hi = [sb(f"x_hi{p}", [P, KT, 512], F32R) for p in range(2)]
        x_lo = [sb(f"x_lo{p}", [P, KT, 512], F32R) for p in range(2)]
        a_act = sb("a_act", [P, 2, 512])
        b_act = sb("b_act", [P, 2, 512])
        c_act = sb("c_act", [P, 2, 512])
        h_hi = sb("h_hi", [P, HT, 512], F32R)
        h_lo = sb("h_lo", [P, HT, 512], F32R)
        f_hi = [sb(f"f_hi{p}", [P, KT, 512], F32R) for p in range(2)]
        f_lo = [sb(f"f_lo{p}", [P, KT, 512], F32R) for p in range(2)]
        y = [sb(f"y{p}", [P, TT, H]) for p in range(2)]
        stats = sb("stats", [P, TT, 6])
        diff, diff2, m2, mean_h = (sb(n, [P, TT]) for n in ("diff", "diff2", "m2", "mean_h"))
        neg_mean = [sb(f"neg_mean{p}", [P, TT]) for p in range(2)]
        hvar = [sb(f"hvar{p}", [P, TT]) for p in range(2)]
        half = sb("half", [P, TT])
        rstd = [sb(f"rstd{p}", [P, TT]) for p in range(2)]
        shift = [sb(f"shift{p}", [P, TT]) for p in range(2)]
        o = [sb(f"o{p}", [P, TT, H]) for p in range(RING)]

        def bank(name):
            return ctx.enter_context(nc.psum_tensor(name, [P, 512], F32))

        ps_a = [bank(f"ps_a{m}") for m in range(2)]
        ps_b = [bank(f"ps_b{m}") for m in range(2)]
        ps_x = [bank(f"ps_x{m}") for m in range(KT)]
        ps_f = [bank(f"ps_f{m}") for m in range(2)]

        cond_in = sem("cond_in")
        w_in = [sem(f"w_in{i}") for i in range(7)]
        rows_in = sem("rows_in")
        bcast_in = sem("bcast_in")
        rows_zero = sem("rows_zero")
        consts = sem("consts")
        dve_step = sem("dve_step")
        w_hi_done = sem("w_hi_done")
        w_lo_done = sem("w_lo_done")
        rows_t = sem("rows_t")
        bias_done = sem("bias_done")
        groups_done = sem("groups_done")
        bounds_ps = sem("bounds_ps")
        place_done = sem("place_done")
        place_ps = sem("place_ps")
        onehot_done = sem("onehot_done")
        rows_ps = sem("rows_ps")
        rows_done = sem("rows_done")
        bf_in = sem("bf_in")
        bf_done = sem("bf_done")
        tabs_ps = sem("tabs_ps")
        tabs_done = sem("tabs_done")
        pool_step = sem("pool_step")
        x_loaded = [sem(f"x_loaded{p}") for p in range(RING)]
        row_done = sem("row_done")
        xT_ready = sem("xT_ready")
        x_hi_done = sem("x_hi_done")
        x_lo_done = sem("x_lo_done")
        a_ready, b_ready, c_ready = sem("a_ready"), sem("b_ready"), sem("c_ready")
        a_gelu, b_gelu, c_gelu = sem("a_gelu"), sem("b_gelu"), sem("c_gelu")
        a_split, b_split, f_split = sem("a_split"), sem("b_split"), sem("f_split")
        f_ready = sem("f_ready")
        y_done = sem("y_done")
        bn_done = sem("bn_done")
        mv_done = sem("mv_done")
        rstd_done = sem("rstd_done")
        z_done = sem("z_done")
        gam_pool, gam_dve = sem("gam_pool"), sem("gam_dve")
        rstd_step = sem("rstd_step")
        gamma_done = sem("gamma_done")
        agg_step = sem("agg_step")
        o_pool, o_dve = sem("o_pool"), sem("o_dve")
        sp_turn, pool_turn = sem("sp_turn"), sem("pool_turn")
        stored = [sem(f"stored{p}") for p in range(RING)]

        AHEAD = 3
        POOL_TT = TT - 1
        CONSTS = 12

        def upto(g, per=1, k=None):
            return (g + AHEAD) * per + (per if k is None else k + 1)


        W_PARTS = [
            (w1_raw[:, :, 0:512], w1_sr.rearrange("(k p) n -> p k n", p=P),
             w1_hi[:, :, 0:512], w1_lo[:, :, 0:512]),
            (w2_raw[:, :, :], w2_sr.rearrange("(k p) n -> p k n", p=P), w2_hi[:, :, :], w2_lo[:, :, :]),
            (w1_raw[:, :, 512:768], w1_nr.rearrange("(k p) n -> p k n", p=P),
             w1_hi[:, :, 512:768], w1_lo[:, :, 512:768]),
            (w1_raw[:, :, 768:1024], w1_tsr.rearrange("(k p) n -> p k n", p=P),
             w1_hi[:, :, 768:1024], w1_lo[:, :, 768:1024]),
        ]
        for r, w in ((SR, w3_sr), (NR, w2_nr), (TSR, w2_tsr)):
            cols = slice(r * KT * H, (r + 1) * KT * H)
            W_PARTS.append((wf_raw[:, r], w.rearrange("(k p) n -> p k n", p=P),
                            wf_hi[:, cols].rearrange("p (k n) -> p k n", k=KT),
                            wf_lo[:, cols].rearrange("p (k n) -> p k n", k=KT)))
        L1_COL = {SR: 0, NR: 512, TSR: 768}

        bounds_pt = ps_a[0][0:ROUTES, 0:2]
        place_pt = ps_a[1][0:B, 0:1]
        perm_pt = ps_f[0][0:1, 0:PLACES]
        cls_pt = ps_f[1][0:1, 0:CLS]
        bias_pt = ps_b[0][:, 0:16]
        rows_pt = ps_b[1][:, 0:CLS]

        block = ctx.enter_context(nc.Block())

        def spread(row, tiles):
            return row[:, :].rearrange("p (a h) -> p a h", a=1).broadcast_to([P, tiles, H])

        def register_set(eng, name, n):
            return [eng.alloc_register(f"{name}{j}") for j in range(n)]

        def load_values(eng, regs, table, at, hi):
            eng.load(regs, table[0:1, bass.ds(at, len(regs))])
            return [eng.snap(r, min_val=0, max_val=hi) for r in regs]

        @block.sync
        def _(sp):
            sp.dma_start(cond_b[:, :], cond.rearrange("(a b) -> a b", a=1).broadcast_to([ROUTES, B])
                         ).then_inc(cond_in, 16)
            for i, (raw, src, _, _) in enumerate(W_PARTS):
                sp.dma_start(raw, src).then_inc(w_in[i], 16)

            idx = register_set(sp, "sp_idx", PER)
            used = register_set(sp, "sp_used", PER)
            cls_regs = register_set(sp, "sp_cls", WINDOW)
            sp.wait_ge(tabs_done, 1)
            with sp.Fori(0, ROUNDS) as i:
                cls = load_values(sp, cls_regs, cls_tab, i * RING, EMPTY)
                for p in range(RING):
                    g = i * RING + p
                    with sp.If(cls[p] < EMPTY):
                        sp.wait_ge(o_pool, upto(g - 2))
                        sp.wait_ge(o_dve, upto(g - 2))
                        sp.sem_inc(sp_turn, 1)
                        taken = load_values(sp, used, store_tab, g * PER, B)
                        for j, s in enumerate(load_values(sp, idx, load_tab, g * PER, B - 1)):
                            sp.dma_start(out[bass.ds(s, 1), :, :].rearrange("a (q t) h -> (a q) t h", t=TT),
                                         o[p][j * ROWS:(j + 1) * ROWS, :, :], cond=(taken[j] > 0)
                                         ).then_inc(stored[p], 16)
                    with sp.Else():
                        sp.sem_inc(stored[p], 16 * PER)
            for p in range(RING):
                sp.wait_ge(stored[p], 16 * PER * ROUNDS)

        @block.gpsimd
        def _(pool):
            nc.gpsimd.memset(ident[:, :], 0.0).then_inc(pool_step, 1)
            nc.gpsimd.memset(tri[:, :, :], 1.0).then_inc(pool_step, 1)
            nc.gpsimd.memset(bias_rows[:, :], 0.0).then_inc(pool_step, 1)
            nc.gpsimd.iota(route_id[:, :], [[0, 1]], base=0, channel_multiplier=1,
                           allow_small_or_imprecise_dtypes=True).then_inc(consts, 1)
            nc.gpsimd.iota(full[:, :], [[PER, B // PER]], base=0, channel_multiplier=0,
                           allow_small_or_imprecise_dtypes=True).then_inc(consts, 1)
            nc.gpsimd.iota(step_id[:, :], [[1, CLS]], base=-2, channel_multiplier=0,
                           allow_small_or_imprecise_dtypes=True).then_inc(consts, 1)
            nc.gpsimd.iota(seq1[:, :], [[0, 1]], base=1, channel_multiplier=1,
                           allow_small_or_imprecise_dtypes=True).then_inc(consts, 1)
            nc.gpsimd.iota(place_id[:, :], [[1, PLACES]], base=-2 * PER, channel_multiplier=0,
                           allow_small_or_imprecise_dtypes=True).then_inc(consts, 1)
            nc.gpsimd.iota(first_place[:, :], [[PER, CLS + 1]], base=0, channel_multiplier=0,
                           allow_small_or_imprecise_dtypes=True).then_inc(consts, 1)
            nc.gpsimd.iota(row_place[:, :], [[1, PER], [0, ROWS]], base=0, channel_multiplier=0,
                           allow_small_or_imprecise_dtypes=True).then_inc(consts, 1)
            nc.gpsimd.iota(row_1[:, :], [[0, PER], [1, ROWS]], base=1, channel_multiplier=ROWS,
                           allow_small_or_imprecise_dtypes=True).then_inc(consts, 1)
            nc.gpsimd.iota(minus_row[:, :], [[0, 1]], base=0, channel_multiplier=-1,
                           allow_small_or_imprecise_dtypes=True).then_inc(consts, 1)
            pool.wait_ge(pool_step, 3)
            for e in range(2):
                nc.gpsimd.affine_select(out=tri[:, e, :], in_=tri[:, e, :], compare_op=ALU.is_ge, fill=0.0,
                                        base=e - 1, pattern=[[1, ROUTES]], channel_multiplier=-1
                                        ).then_inc(consts, 1)
            nc.gpsimd.affine_select(out=ident[:, :], in_=ident[:, :], compare_op=ALU.not_equal, fill=1.0,
                                    base=0, pattern=[[-1, P]], channel_multiplier=1).then_inc(consts, 1)
            nc.gpsimd.memset(half[:, :], -0.5).then_inc(pool_step, 1)
            nc.gpsimd.memset(bf_raw[:, NONE * H:(NONE + 1) * H], 0.0).then_inc(bf_in, 16)
            nc.gpsimd.memset(ones2[:, :].bitcast(F32), 1.0).then_inc(bf_in, 16)

            x_rows = x.rearrange("b (q t) h -> (b q) (t h)", t=TT)

            def gather(p, index):
                nc.gpsimd.indirect_dma_start(
                    out=x_in[p][:, :, :].rearrange("p t h -> p (t h)"), out_offset=None, in_=x_rows,
                    in_offset=bass.IndirectOffsetOnAxis(ap=index, axis=0)).then_inc(x_loaded[p], 16)

            pool.wait_ge(rows_done, 1)
            gather(0, row_idx[:, 0:1])
            gather(1, row_idx[:, 1:2])
            gather(2, row_idx[:, 2:3])
            pool.wait_ge(pool_step, 4)
            pool.wait_ge(bcast_in, 16 * 2)
            nc.gpsimd.tensor_scalar(gamma_b[:, :], gamma_b[:, :], float(H) ** 0.5, None, ALU.mult
                                    ).then_inc(gamma_done, 1)
            pool.wait_ge(gamma_done, 1)

            for done, per in ((gam_pool, 1), (o_pool, 1), (row_done, 1), (rstd_step, 1), (rstd_done, 1)):
                pool.sem_inc(done, AHEAD * per)
            cls_regs = register_set(pool, "pool_cls", WINDOW)
            pool.wait_ge(tabs_done, 1)
            with pool.Fori(0, ROUNDS) as i:
                cls = load_values(pool, cls_regs, cls_tab, i * RING, EMPTY)
                for p in range(RING):
                    g = i * RING + p
                    with pool.If(cls[5 + p] < EMPTY):
                        nxt = (p + 3) % RING
                        nc.gpsimd.tensor_copy(row_cur[:, nxt:nxt + 1], row_idx[:, bass.ds(g + 3, 1)]
                                              ).then_inc(row_done, 1)
                        pool.wait_ge(y_done, upto(g - 1, 2))
                        pool.wait_ge(row_done, upto(g))
                        pool.sem_inc(pool_turn, 1)
                        gather(nxt, row_cur[:, nxt:nxt + 1])
                    with pool.If(cls[1 + p] < EMPTY):
                        q = (p + 1) % 2
                        pool.wait_ge(mv_done, upto(g - 1))
                        nc.gpsimd.tensor_tensor(rstd[q][:, :], hvar[q][:, :], half[:, :], ALU.pow
                                                ).then_inc(rstd_step, 1)
                        pool.wait_ge(rstd_step, upto(g - 1))
                        nc.gpsimd.tensor_tensor(shift[q][:, :], rstd[q][:, :], neg_mean[q][:, :], ALU.mult
                                                ).then_inc(rstd_done, 1)
                    with pool.If(cls[p] < EMPTY):
                        pool.wait_ge(z_done, upto(g - 2))
                        nc.gpsimd.tensor_tensor(o[p][:, 0:POOL_TT, :], o[p][:, 0:POOL_TT, :],
                                                spread(gamma_b, POOL_TT), ALU.mult).then_inc(gam_pool, 1)
                        pool.wait_ge(gam_pool, upto(g - 2))
                        nc.gpsimd.tensor_tensor(o[p][:, 0:POOL_TT, :], o[p][:, 0:POOL_TT, :],
                                                spread(beta_b, POOL_TT), ALU.add).then_inc(o_pool, 1)

        @block.scalar
        def _(act):
            act.wait_ge(consts, CONSTS)
            act.wait_ge(pool_step, 3)
            for row, b in ((0, b1_sr), (4 * NR, b1_nr), (4 * TSR, b1_tsr), (14, b2_sr)):
                n = b.shape[0] // P
                act.dma_start(bias_rows[row:row + n, :], b.rearrange("(m p) -> m p", p=P)).then_inc(rows_in, 16)
            for r, b in ((SR, b3_sr), (NR, b2_nr), (TSR, b2_tsr)):
                act.dma_start(bf_raw[:, r * H:(r + 1) * H], b.rearrange("(a n) -> a n", a=1).broadcast_to([2, H])
                              ).then_inc(bf_in, 16)
            for dst, b in ((gamma_b, gamma), (beta_b, beta)):
                act.dma_start(dst[:, :], b.rearrange("(a n) -> a n", a=1).broadcast_to([P, H])
                              ).then_inc(bcast_in, 16)
            nc.scalar.activation(warm[:, :], ident[0:1, 0:1], ACT.Gelu)
            for i, (raw, _, hi, _) in enumerate(W_PARTS):
                act.wait_ge(w_in[i], 16)
                nc.scalar.activation(hi, raw, ACT.Copy).then_inc(w_hi_done, 1)
            for done, per in ((x_hi_done, KT), (a_gelu, 2), (b_gelu, 2), (c_gelu, 2), (z_done, 1)):
                act.sem_inc(done, AHEAD * per)
            act.wait_ge(bias_done, 1)

            def x_high(g, p):
                for kt in range(KT):
                    act.wait_ge(xT_ready, upto(g, KT, kt))
                    nc.scalar.activation(x_hi[p][:, kt, :], ps_x[kt][:, :], ACT.Copy).then_inc(x_hi_done, 1)

            x_high(0, 0)
            cls_regs = register_set(act, "act_cls", WINDOW)

            def gelu(src, full, hi, bias, done):
                nc.scalar.activation(full, src, ACT.Gelu, bias=bias)
                nc.scalar.activation(hi, src, ACT.Gelu, bias=bias).then_inc(done, 1)

            act.wait_ge(tabs_done, 1)
            with act.Fori(0, ROUNDS) as i:
                cls = load_values(act, cls_regs, cls_tab, i * RING, EMPTY)
                for p in range(RING):
                    g = i * RING + p
                    with act.If(cls[3 + p] < EMPTY):
                        x_high(g + 1, (p + 1) % 2)
                    with act.If(cls[2 + p] < NR):
                        for m in range(2):
                            act.wait_ge(a_ready, upto(g, 2, m))
                            act.wait_ge(f_split, upto(g - 1, 2, m))
                            gelu(ps_a[m][:, :], a_act[:, m, :], h_hi[:, m, :], bias_cols[:, m:m + 1], a_gelu)
                        for m in range(2):
                            act.wait_ge(b_ready, upto(g, 2, m))
                            gelu(ps_b[m][:, :], b_act[:, m, :], h_hi[:, 2 + m, :],
                                 bias_cols[:, 2 + m:3 + m], b_gelu)
                    with act.Else():
                        with act.If(cls[2 + p] < EMPTY):
                            bias_at = act.snap(cls[2 + p].with_bounds(max_val=NONE) * 4)
                            for m in range(2):
                                act.wait_ge(a_ready, upto(g, 2, m))
                                act.wait_ge(f_split, upto(g - 1, 2, m))
                                gelu(ps_a[m][:, :], a_act[:, m, :], f_hi[p % 2][:, m, :],
                                     bias_cols[:, bass.ds(bias_at + m, 1)], a_gelu)
                    with act.If(cls[p] < EMPTY):
                        act.wait_ge(rstd_done, upto(g - 2))
                        act.wait_ge(stored[p], 16 * PER * i)
                        for t in range(TT):
                            z = nc.scalar.activation(o[p][:, t, :], y[p % 2][:, t, :], ACT.Identity,
                                                     bias=shift[p % 2][:, t:t + 1], scale=rstd[p % 2][:, t:t + 1])
                        z.then_inc(z_done, 1)
                    with act.If(cls[2 + p] < NR):
                        for m in range(2):
                            act.wait_ge(c_ready, upto(g, 2, m))
                            gelu(ps_b[m][:, :], c_act[:, m, :], f_hi[p % 2][:, m, :],
                                 bias_cols[:, 14 + m:15 + m], c_gelu)

        @block.vector
        def _(dve):
            step = [0]

            def chain(ins):
                step[0] += 1
                ins.then_inc(dve_step, 1)
                dve.wait_ge(dve_step, step[0])

            chain(nc.vector.memset(ones4[:, :], 1.0))
            chain(nc.vector.memset(zeros[:, :], 0.0))
            dve.wait_ge(cond_in, 16)
            chain(nc.vector.tensor_copy(cond_f[:, :], cond_b[:, :]))
            for j, (value, less) in enumerate(((2, NONE - SR), (0, NONE - NR), (1, NONE - TSR))):
                chain(nc.vector.tensor_scalar(key[:, j, :], cond_f[:, :], float(value), float(-less),
                                              ALU.is_equal, ALU.mult))
            chain(nc.vector.tensor_tensor(key[:, 0, :], key[:, 0, :], key[:, 1, :], ALU.add))
            chain(nc.vector.scalar_tensor_tensor(out=key[:, 1, :], in0=key[:, 0, :], scalar=float(NONE),
                                                 in1=key[:, 2, :], op0=ALU.add, op1=ALU.add))
            dve.wait_ge(consts, CONSTS)
            chain(nc.vector.tensor_scalar(onehot[:, :], key[:, 1, :], route_id[:, 0:1], None, ALU.is_equal))
            chain(nc.vector.tensor_tensor_scan(rank[:, :], onehot[:, :], zeros[:, :], 0.0, ALU.add, ALU.add))
            chain(nc.vector.tensor_scalar(over[:, :], full[:, :], rank[:, B - 1:B], None, ALU.is_lt))
            nc.vector.tensor_reduce(groups[:, :], over[:, :], AX.X, ALU.add).then_inc(groups_done, 1)
            dve.wait_ge(bounds_ps, 1)
            chain(nc.vector.tensor_copy(bounds[:, :], bounds_pt))
            chain(nc.vector.tensor_scalar(place_m[:, 0, :], rank[:, :], -1.0, None, ALU.add))
            chain(nc.vector.tensor_scalar(bounds[:, 0:1], bounds[:, 0:1], float(PER), None, ALU.mult))
            chain(nc.vector.tensor_scalar(place_m[:, 0, :], place_m[:, 0, :], bounds[:, 0:1], None, ALU.add))
            nc.vector.tensor_tensor(place_m[:, 1, :], place_m[:, 0, :], onehot[:, :], ALU.mult
                                    ).then_inc(place_done, 1)
            chain(nc.vector.tensor_scalar(ended[:, 0, :], step_id[:, :], bounds[:, 1:2], None, ALU.is_ge))
            chain(nc.vector.tensor_scalar(ended[:, 1, :], step_id[:, :], 0.0, None, ALU.is_lt))
            chain(nc.vector.tensor_tensor(ended[:, 0, :], ended[:, 0, :], ended[:, 1, :], ALU.add))
            dve.wait_ge(place_ps, 1)
            chain(nc.vector.tensor_copy(place_col[:, :], place_pt))
            chain(nc.vector.tensor_scalar(reached[:, :], first_place[:, :], place_col[:, 0:1], None, ALU.is_le))
            chain(nc.vector.tensor_tensor(in_group[:, :], reached[:, 0:CLS], reached[:, 1:CLS + 1], ALU.subtract))
            chain(nc.vector.tensor_reduce(nth_group[:, :], reached[:, 1:CLS + 1], AX.X, ALU.add))
            chain(nc.vector.scalar_tensor_tensor(out=in_place[:, :], in0=nth_group[:, :], scalar=-float(PER),
                                                 in1=place_col[:, :], op0=ALU.mult, op1=ALU.add))
            nc.vector.scalar_tensor_tensor(out=row_at[:, :], in0=row_place[:, :], scalar=in_place[:, 0:1],
                                           in1=row_1[:, :], op0=ALU.is_equal, op1=ALU.mult
                                           ).then_inc(onehot_done, 1)
            nc.vector.tensor_scalar(at_place[:, :], place_id[:, :], place_col[:, 0:1], None, ALU.is_equal
                                    ).then_inc(onehot_done, 1)
            dve.wait_ge(rows_ps, 1)
            chain(nc.vector.tensor_scalar(row_f[:, :], rows_pt, -1.0, 0.0, ALU.add, ALU.max))
            nc.vector.tensor_copy(row_idx[:, :], row_f[:, :]).then_inc(rows_done, 1)
            dve.wait_ge(tabs_ps, 1)
            nc.vector.tensor_copy(cls_tab[:, :], cls_pt)
            nc.vector.tensor_copy(store_tab[:, :], perm_pt)
            chain(nc.vector.tensor_scalar(load_f[:, :], perm_pt, -1.0, 0.0, ALU.add, ALU.max))
            nc.vector.tensor_copy(load_tab[:, :], load_f[:, :]).then_inc(tabs_done, 1)

            dve.wait_ge(rows_t, 1)
            nc.vector.tensor_copy(bias_cols[:, :], bias_pt).then_inc(bias_done, 1)
            for w in (wf_hi, wf_lo):
                nc.vector.memset(w[:, NONE * KT * H:(NONE + 1) * KT * H].bitcast(F32), 0.0)
            for i, (raw, _, hi, lo) in enumerate(W_PARTS):
                dve.wait_ge(w_hi_done, i + 1)
                nc.vector.tensor_tensor(lo, raw, hi.bitcast(F32), ALU.subtract).then_inc(w_lo_done, 1)
            dve.wait_ge(bf_in, 16 * 5)
            chain(nc.vector.tensor_copy(bf_round[:, :], bf_raw[:, :]))
            nc.vector.scalar_tensor_tensor(out=bf_parts[:, :], in0=bf_round[:, :].bitcast(F32),
                                           scalar=minus_row[:, 0:1], in1=bf_raw[:, :], op0=ALU.mult, op1=ALU.add
                                           ).then_inc(bf_done, 1)
            dve.wait_ge(gamma_done, 1)
            for done, per in ((x_lo_done, KT), (a_split, 2), (b_split, 2), (f_split, 2), (gam_dve, 1), (o_dve, 1),
                              (y_done, 2), (bn_done, TT), (agg_step, 4), (mv_done, 1)):
                dve.sem_inc(done, AHEAD * per)

            def x_low(g, p):
                for kt in range(KT):
                    dve.wait_ge(x_hi_done, upto(g, KT, kt))
                    nc.vector.tensor_tensor(x_lo[p][:, kt, :], ps_x[kt][:, :], x_hi[p][:, kt, :].bitcast(F32),
                                            ALU.subtract).then_inc(x_lo_done, 1)

            def low(src, hi, lo, done):
                nc.vector.tensor_tensor(lo, src, hi.bitcast(F32), ALU.subtract).then_inc(done, 1)

            x_low(0, 0)
            cls_regs = register_set(dve, "dve_cls", WINDOW)
            with dve.Fori(0, ROUNDS) as i:
                cls = load_values(dve, cls_regs, cls_tab, i * RING, EMPTY)
                for p in range(RING):
                    g = i * RING + p
                    with dve.If(cls[3 + p] < EMPTY):
                        x_low(g + 1, (p + 1) % 2)
                    with dve.If(cls[2 + p] < NR):
                        for m in range(2):
                            dve.wait_ge(a_gelu, upto(g, 2, m))
                            low(a_act[:, m, :], h_hi[:, m, :], h_lo[:, m, :], a_split)
                        for m in range(2):
                            dve.wait_ge(b_gelu, upto(g, 2, m))
                            low(b_act[:, m, :], h_hi[:, 2 + m, :], h_lo[:, 2 + m, :], b_split)
                    with dve.Else():
                        with dve.If(cls[2 + p] < EMPTY):
                            for m in range(2):
                                dve.wait_ge(a_gelu, upto(g, 2, m))
                                low(a_act[:, m, :], f_hi[p % 2][:, m, :], f_lo[p % 2][:, m, :], f_split)
                    with dve.If(cls[1 + p] < EMPTY):
                        q = (p + 1) % 2
                        dve.wait_ge(z_done, upto(g - 3))
                        for b in range(2):
                            dve.wait_ge(f_ready, upto(g - 1, 2, b))
                            nc.vector.tensor_tensor(
                                y[q][:, 2 * b:2 * b + 2, :], ps_f[b][:, :].rearrange("p (t h) -> p t h", t=2),
                                x_in[(p - 1) % RING][:, 2 * b:2 * b + 2, :], ALU.add).then_inc(y_done, 1)
                        for t in range(TT):
                            dve.wait_ge(y_done, upto(g - 1, 2, t // 2))
                            nc.vector.bn_stats(stats[:, t, :], y[q][:, t, :]).then_inc(bn_done, 1)
                        mean_e, m2_e, mean_o, m2_o = (stats[:, :, c] for c in (1, 2, 4, 5))
                        dve.wait_ge(bn_done, upto(g - 1, TT))
                        nc.vector.tensor_tensor(diff[:, :], mean_e, mean_o, ALU.subtract).then_inc(agg_step, 1)
                        nc.vector.tensor_tensor(m2[:, :], m2_e, m2_o, ALU.add).then_inc(agg_step, 1)
                        nc.vector.tensor_scalar(mean_h[:, :], mean_e, -0.5, None, ALU.mult).then_inc(agg_step, 1)
                        dve.wait_ge(agg_step, upto(g - 1, 4, 0))
                        nc.vector.scalar_tensor_tensor(out=diff2[:, :], in0=diff[:, :], scalar=H / 4.0,
                                                       in1=diff[:, :], op0=ALU.mult, op1=ALU.mult
                                                       ).then_inc(agg_step, 1)
                        dve.wait_ge(agg_step, upto(g - 1, 4, 2))
                        nc.vector.scalar_tensor_tensor(out=neg_mean[q][:, :], in0=mean_o, scalar=-0.5,
                                                       in1=mean_h[:, :], op0=ALU.mult, op1=ALU.add)
                        dve.wait_ge(agg_step, upto(g - 1, 4, 3))
                        nc.vector.scalar_tensor_tensor(out=hvar[q][:, :], in0=m2[:, :], scalar=H * EPS,
                                                       in1=diff2[:, :], op0=ALU.add, op1=ALU.add
                                                       ).then_inc(mv_done, 1)
                    with dve.If(cls[p] < EMPTY):
                        dve.wait_ge(z_done, upto(g - 2))
                        last = o[p][:, POOL_TT, :]
                        nc.vector.tensor_tensor(last, last, gamma_b[:, :], ALU.mult).then_inc(gam_dve, 1)
                        dve.wait_ge(gam_dve, upto(g - 2))
                        nc.vector.tensor_tensor(last, last, beta_b[:, :], ALU.add).then_inc(o_dve, 1)
                    with dve.If(cls[2 + p] < NR):
                        for m in range(2):
                            dve.wait_ge(c_gelu, upto(g, 2, m))
                            low(c_act[:, m, :], f_hi[p % 2][:, m, :], f_lo[p % 2][:, m, :], f_split)

        @block.tensor
        def _(pe):
            pe.wait_ge(consts, CONSTS)
            pe.wait_ge(groups_done, 1)
            for e in range(2):
                mm = nc.tensor.matmul(bounds_pt[:, e:e + 1], tri[:, e, :], groups[:, :], start=True, stop=True)
            mm.then_inc(bounds_ps, 1)
            pe.wait_ge(place_done, 1)
            nc.tensor.matmul(place_pt, place_m[:, 1, :], ones4[:, :], start=True, stop=True).then_inc(place_ps, 1)
            pe.wait_ge(onehot_done, 1)
            nc.tensor.matmul(rows_pt, row_at[:, :], in_group[:, :], start=True, stop=True).then_inc(rows_ps, 1)
            pe.wait_ge(onehot_done, 2)
            nc.tensor.matmul(perm_pt, seq1[:, :], at_place[:, :], start=True, stop=True)
            nc.tensor.matmul(cls_pt, ones4[:, :], ended[:, 0, :], start=True, stop=True).then_inc(tabs_ps, 1)
            pe.wait_ge(rows_in, 16 * 4)
            nc.tensor.transpose(bias_pt, bias_rows[:, :], ident[0:16, 0:16]).then_inc(rows_t, 1)

            def transpose_x(g, p, nth):
                pe.wait_ge(x_loaded[p], 16 * nth)
                for kt in range(KT):
                    for t in range(TT):
                        mm = nc.tensor.transpose(ps_x[kt][:, t * P:(t + 1) * P],
                                                 x_in[p][:, t, kt * P:(kt + 1) * P], ident[:, :])
                    mm.then_inc(xT_ready, 1)

            def layer1(route, m, p, dst):
                cols = slice(L1_COL[route] + m * P, L1_COL[route] + (m + 1) * P)
                for kt in range(KT):
                    nc.tensor.matmul(dst, w1_lo[:, kt, cols], x_hi[p % 2][:, kt, :], start=(kt == 0), stop=False)
                    nc.tensor.matmul(dst, w1_hi[:, kt, cols], x_lo[p % 2][:, kt, :], start=False, stop=False)
                    mm = nc.tensor.matmul(dst, w1_hi[:, kt, cols], x_hi[p % 2][:, kt, :], start=False,
                                          stop=(kt == KT - 1))
                return mm

            def layer1_a(route, g, p):
                for m in range(2):
                    pe.wait_ge(a_gelu, upto(g - 1, 2, m))
                    layer1(route, m, p, ps_a[m][:, :]).then_inc(a_ready, 1)

            for done, per in ((xT_ready, KT), (a_ready, 2), (b_ready, 2), (c_ready, 2), (f_ready, 2)):
                pe.sem_inc(done, AHEAD * per)
            pe.wait_ge(bias_done, 1)
            pe.wait_ge(bf_done, 1)
            pe.wait_ge(tabs_done, 1)
            transpose_x(0, 0, 1)
            pe.wait_ge(w_lo_done, len(W_PARTS))
            cls_regs = register_set(pe, "pe_cls", WINDOW)
            with pe.Fori(0, ROUNDS) as i:
                cls = load_values(pe, cls_regs, cls_tab, i * RING, EMPTY)
                for p in range(RING):
                    g = i * RING + p
                    with pe.If(cls[2 + p] < EMPTY):
                        pe.wait_ge(x_lo_done, upto(g, KT))
                        with pe.If(cls[3 + p] < EMPTY):
                            transpose_x(g + 1, (p + 1) % RING, i + 1 + (p + 1) // RING)
                        with pe.If(cls[2 + p] < NR):
                            layer1_a(SR, g, p)
                            for m in range(2):
                                if m == 0:
                                    pe.wait_ge(c_gelu, upto(g - 1, 2))
                                layer1(SR, 2 + m, p, ps_b[m][:, :]).then_inc(b_ready, 1)
                        with pe.Else():
                            with pe.If(cls[2 + p] < TSR):
                                layer1_a(NR, g, p)
                            with pe.Else():
                                layer1_a(TSR, g, p)
                    with pe.If(cls[1 + p] < EMPTY):
                        q = (p + 1) % 2
                        pe.wait_ge(f_split, upto(g - 1, 2))
                        f_at = pe.snap(cls[1 + p].with_bounds(max_val=NONE) * (KT * H))
                        b_at = pe.snap(cls[1 + p].with_bounds(max_val=NONE) * H)
                        for t in range(TT):
                            dst = ps_f[t // 2][:, (t % 2) * H:(t % 2 + 1) * H]
                            if t % 2 == 0:
                                pe.wait_ge(y_done, upto(g - 2, 2, t // 2))
                            for kt in range(KT):
                                toks = slice(t * P, (t + 1) * P)
                                w_hi = wf_hi[:, bass.ds(f_at + kt * H, H)]
                                w_lo = wf_lo[:, bass.ds(f_at + kt * H, H)]
                                nc.tensor.matmul(dst, f_lo[q][:, kt, toks], w_hi, start=(kt == 0), stop=False)
                                nc.tensor.matmul(dst, f_hi[q][:, kt, toks], w_lo, start=False, stop=False)
                                nc.tensor.matmul(dst, f_hi[q][:, kt, toks], w_hi, start=False, stop=False)
                            mm = nc.tensor.matmul(dst, ones2[:, :], bf_parts[:, bass.ds(b_at, H)],
                                                  start=False, stop=True)
                            if t % 2:
                                mm.then_inc(f_ready, 1)
                    with pe.If(cls[2 + p] < NR):
                        for m in range(2):
                            dst = ps_b[m][:, :]
                            cols = slice(m * P, (m + 1) * P)
                            pe.wait_ge(b_gelu, upto(g, 2, m))
                            for kt in range(HT):
                                if m == 0 and kt == 0:
                                    pe.wait_ge(a_split, upto(g, 2))
                                if m == 0 and kt >= 2:
                                    pe.wait_ge(b_split, upto(g, 2, kt - 2))
                                nc.tensor.matmul(dst, w2_lo[:, kt, cols], h_hi[:, kt, :], start=(kt == 0),
                                                 stop=False)
                                nc.tensor.matmul(dst, w2_hi[:, kt, cols], h_lo[:, kt, :], start=False,
                                                 stop=False)
                                mm = nc.tensor.matmul(dst, w2_hi[:, kt, cols], h_hi[:, kt, :], start=False,
                                                      stop=(kt == HT - 1))
                            mm.then_inc(c_ready, 1)


INPUTS = ["x", "itok_B_0_2"] + ["L0_cond_" + n for n in (
    "w1_nr", "b1_nr", "w2_nr", "b2_nr", "w1_tsr", "b1_tsr", "w2_tsr", "b2_tsr",
    "w1_sr", "b1_sr", "w2_sr", "b2_sr", "w3_sr", "b3_sr", "gamma", "beta")]


def kernel(**inputs):
    import numpy as np
    import concourse.bacc as bacc
    from concourse.bass_utils import run_bass_kernel_spmd

    nc = bacc.Bacc("TRN2", target_bir_lowering=False, num_devices=1)
    arrays, args = {}, []
    for name in INPUTS:
        a = np.ascontiguousarray(inputs[name])
        arrays[f"{name}_dram"] = a
        args.append(nc.dram_tensor(f"{name}_dram", a.shape, mybir.dt.from_np(a.dtype), kind="ExternalInput").ap())
    args.append(nc.dram_tensor("out_dram", inputs["x"].shape, F32, kind="ExternalOutput").ap())
    build_cond_mlp(nc, *args)
    result = run_bass_kernel_spmd(nc, [arrays], core_ids=[0])
    return result.results[0]["out_dram"]
```

```python
from contextlib import ExitStack

import concourse.bass as bass
from concourse import mybir

ALU = mybir.AluOpType
ACT = mybir.ActivationFunctionType
AX = mybir.AxisListType
F32 = mybir.dt.float32
F32R = mybir.dt.float32r
I32 = mybir.dt.int32

P = 128
EPS = 1e-5
SR, NR, TSR, NONE, EMPTY = range(5)


def build_cond_mlp(nc, x, cond, w1_nr, b1_nr, w2_nr, b2_nr, w1_tsr, b1_tsr, w2_tsr, b2_tsr,
                   w1_sr, b1_sr, w2_sr, b2_sr, w3_sr, b3_sr, gamma, beta, out):
    B, T, H = x.shape
    KT = H // P
    HT = w1_sr.shape[1] // P
    PER = 512 // T
    TT = PER * T // P
    ROWS = P // PER
    ROUTES = 4
    SLOTS = B // PER + ROUTES - 1
    STEPS = SLOTS + 2
    RING = 4
    ROUNDS = -(-STEPS // RING)
    STORE_ROUNDS = -(-SLOTS // RING)
    WINDOW = RING + 5
    CLS = RING * ROUNDS + 5
    PLACES = CLS * PER
    assert KT == 2 and HT == 4 and TT * ROWS == T and TT == 4

    with ExitStack() as ctx:
        def sb(name, shape, dt=F32):
            return ctx.enter_context(nc.sbuf_tensor(name, shape, dt))

        def sem(name):
            return ctx.enter_context(nc.semaphore(name))

        w1_raw = sb("w1_raw", [P, KT, 2 * 512])
        w1_hi = sb("w1_hi", [P, KT, 2 * 512], F32R)
        w1_lo = sb("w1_lo", [P, KT, 2 * 512], F32R)
        w2_raw = sb("w2_raw", [P, HT, H])
        w2_hi = sb("w2_hi", [P, HT, H], F32R)
        w2_lo = sb("w2_lo", [P, HT, H], F32R)
        wf_raw = sb("wf_raw", [P, ROUTES - 1, KT, H])
        wf_hi = sb("wf_hi", [P, ROUTES * KT * H], F32R)
        wf_lo = sb("wf_lo", [P, ROUTES * KT * H], F32R)
        bias_rows = sb("bias_rows", [16, P])
        bias_cols = sb("bias_cols", [P, 16])
        bf_raw = sb("bf_raw", [2, ROUTES * H])
        bf_round = sb("bf_round", [2, ROUTES * H], F32R)
        bf_parts = sb("bf_parts", [2, ROUTES * H], F32R)
        minus_row = sb("minus_row", [2, 1])
        ones2 = sb("ones2", [2, P], F32R)
        gamma_b = sb("gamma_b", [P, H])
        beta_b = sb("beta_b", [P, H])
        ident = sb("ident", [P, P])
        warm = sb("warm", [1, 1])
        cond_b = sb("cond_b", [ROUTES, B], I32)
        cond_f = sb("cond_f", [ROUTES, B])
        key = sb("key", [ROUTES, 3, B])
        onehot = sb("onehot", [ROUTES, B])
        rank = sb("rank", [ROUTES, B])
        zeros = sb("zeros", [ROUTES, B])
        route_id = sb("route_id", [ROUTES, 1])
        full = sb("full", [ROUTES, B // PER])
        over = sb("over", [ROUTES, B // PER])
        groups = sb("groups", [ROUTES, 1])
        tri = sb("tri", [ROUTES, 2, ROUTES])
        bounds = sb("bounds", [ROUTES, 2])
        place_m = sb("place_m", [ROUTES, 2, B])
        ones4 = sb("ones4", [ROUTES, 1])
        step_id = sb("step_id", [ROUTES, CLS])
        ended = sb("ended", [ROUTES, 2, CLS])
        seq1 = sb("seq1", [B, 1])
        place_id = sb("place_id", [B, PLACES])
        place_col = sb("place_col", [B, 1])
        at_place = sb("at_place", [B, PLACES])
        first_place = sb("first_place", [B, CLS + 1])
        reached = sb("reached", [B, CLS + 1])
        in_group = sb("in_group", [B, CLS])
        nth_group = sb("nth_group", [B, 1])
        in_place = sb("in_place", [B, 1])
        row_place = sb("row_place", [B, P])
        row_1 = sb("row_1", [B, P])
        row_at = sb("row_at", [B, P])
        row_f = sb("row_f", [P, CLS])
        row_idx = sb("row_idx", [P, CLS], I32)
        row_cur = sb("row_cur", [P, RING], I32)
        cls_tab = sb("cls_tab", [1, CLS], I32)
        store_tab = sb("store_tab", [1, PLACES], I32)
        load_f = sb("load_f", [1, PLACES])
        load_tab = sb("load_tab", [1, PLACES], I32)
        x_in = [sb(f"x_in{p}", [P, TT, H]) for p in range(RING)]
        x_hi = [sb(f"x_hi{p}", [P, KT, 512], F32R) for p in range(2)]
        x_lo = [sb(f"x_lo{p}", [P, KT, 512], F32R) for p in range(2)]
        a_act = sb("a_act", [P, 2, 512])
        b_act = sb("b_act", [P, 2, 512])
        c_act = sb("c_act", [P, 2, 512])
        h_hi = sb("h_hi", [P, HT, 512], F32R)
        h_lo = sb("h_lo", [P, HT, 512], F32R)
        f_hi = [sb(f"f_hi{p}", [P, KT, 512], F32R) for p in range(2)]
        f_lo = [sb(f"f_lo{p}", [P, KT, 512], F32R) for p in range(2)]
        y = [sb(f"y{p}", [P, TT, H]) for p in range(2)]
        stats = sb("stats", [P, TT, 6])
        diff, diff2, m2, mean_h = (sb(n, [P, TT]) for n in ("diff", "diff2", "m2", "mean_h"))
        neg_mean = [sb(f"neg_mean{p}", [P, TT]) for p in range(2)]
        hvar = [sb(f"hvar{p}", [P, TT]) for p in range(2)]
        half = sb("half", [P, TT])
        rstd = [sb(f"rstd{p}", [P, TT]) for p in range(2)]
        shift = [sb(f"shift{p}", [P, TT]) for p in range(2)]
        o = [sb(f"o{p}", [P, TT, H]) for p in range(RING)]

        def bank(name):
            return ctx.enter_context(nc.psum_tensor(name, [P, 512], F32))

        ps_a = [bank(f"ps_a{m}") for m in range(2)]
        ps_b = [bank(f"ps_b{m}") for m in range(2)]
        ps_x = [bank(f"ps_x{m}") for m in range(KT)]
        ps_f = [bank(f"ps_f{m}") for m in range(2)]

        cond_in = sem("cond_in")
        w_in = [sem(f"w_in{i}") for i in range(7)]
        rows_in = sem("rows_in")
        bcast_in = sem("bcast_in")
        rows_zero = sem("rows_zero")
        consts = sem("consts")
        dve_step = sem("dve_step")
        w_hi_done = sem("w_hi_done")
        w_lo_done = sem("w_lo_done")
        rows_t = sem("rows_t")
        bias_done = sem("bias_done")
        groups_done = sem("groups_done")
        bounds_ps = sem("bounds_ps")
        place_done = sem("place_done")
        place_ps = sem("place_ps")
        onehot_done = sem("onehot_done")
        rows_ps = sem("rows_ps")
        rows_done = sem("rows_done")
        bf_in = sem("bf_in")
        bf_rounded = sem("bf_rounded")
        bf_done = sem("bf_done")
        wf_lo_done = sem("wf_lo_done")
        tabs_ps = sem("tabs_ps")
        tabs_done = sem("tabs_done")
        pool_step = sem("pool_step")
        x_loaded = [sem(f"x_loaded{p}") for p in range(RING)]
        row_done = sem("row_done")
        xT_ready = sem("xT_ready")
        x_hi_done = sem("x_hi_done")
        x_lo_done = sem("x_lo_done")
        a_ready, b_ready, c_ready = sem("a_ready"), sem("b_ready"), sem("c_ready")
        a_gelu, b_gelu, c_gelu = sem("a_gelu"), sem("b_gelu"), sem("c_gelu")
        a_split, b_split, f_split = sem("a_split"), sem("b_split"), sem("f_split")
        f_ready = sem("f_ready")
        y_done = sem("y_done")
        bn_done = sem("bn_done")
        mv_done = sem("mv_done")
        rstd_done = sem("rstd_done")
        z_done = sem("z_done")
        gam_pool, gam_dve = sem("gam_pool"), sem("gam_dve")
        rstd_step = sem("rstd_step")
        gamma_done = sem("gamma_done")
        agg_step = sem("agg_step")
        o_pool, o_dve = sem("o_pool"), sem("o_dve")
        sp_turn, pool_turn = sem("sp_turn"), sem("pool_turn")
        stored = [sem(f"stored{p}") for p in range(RING)]

        AHEAD = 3
        POOL_TT = TT - 1
        CONSTS = 12

        def upto(g, per=1, k=None):
            return (g + AHEAD) * per + (per if k is None else k + 1)


        W_PARTS = [
            (w1_raw[:, :, 0:512], w1_sr.rearrange("(k p) n -> p k n", p=P),
             w1_hi[:, :, 0:512], w1_lo[:, :, 0:512]),
            (w1_raw[:, :, 512:768], w1_nr.rearrange("(k p) n -> p k n", p=P),
             w1_hi[:, :, 512:768], w1_lo[:, :, 512:768]),
            (w1_raw[:, :, 768:1024], w1_tsr.rearrange("(k p) n -> p k n", p=P),
             w1_hi[:, :, 768:1024], w1_lo[:, :, 768:1024]),
            (w2_raw[:, :, :], w2_sr.rearrange("(k p) n -> p k n", p=P), w2_hi[:, :, :], w2_lo[:, :, :]),
        ]
        for r, w in ((SR, w3_sr), (NR, w2_nr), (TSR, w2_tsr)):
            cols = slice(r * KT * H, (r + 1) * KT * H)
            W_PARTS.append((wf_raw[:, r], w.rearrange("(k p) n -> p k n", p=P),
                            wf_hi[:, cols].rearrange("p (k n) -> p k n", k=KT),
                            wf_lo[:, cols].rearrange("p (k n) -> p k n", k=KT)))
        L1_COL = {SR: 0, NR: 512, TSR: 768}
        DVE_PARTS = 4

        bounds_pt = ps_a[0][0:ROUTES, 0:2]
        place_pt = ps_a[1][0:B, 0:1]
        perm_pt = ps_f[0][0:1, 0:PLACES]
        cls_pt = ps_f[1][0:1, 0:CLS]
        bias_pt = ps_b[0][:, 0:16]
        rows_pt = ps_b[1][:, 0:CLS]

        block = ctx.enter_context(nc.Block())

        def spread(row, tiles):
            return row[:, :].rearrange("p (a h) -> p a h", a=1).broadcast_to([P, tiles, H])

        def register_set(eng, name, n):
            return [eng.alloc_register(f"{name}{j}") for j in range(n)]

        def load_values(eng, regs, table, at, hi):
            eng.load(regs, table[0:1, bass.ds(at, len(regs))])
            return [eng.snap(r, min_val=0, max_val=hi) for r in regs]

        @block.sync
        def _(sp):
            sp.dma_start(cond_b[:, :], cond.rearrange("(a b) -> a b", a=1).broadcast_to([ROUTES, B])
                         ).then_inc(cond_in, 16)
            for i, (raw, src, _, _) in enumerate(W_PARTS):
                sp.dma_start(raw, src).then_inc(w_in[i], 16)

            idx = register_set(sp, "sp_idx", PER)
            used = register_set(sp, "sp_used", PER)
            cls_regs = register_set(sp, "sp_cls", RING)
            sp.wait_ge(tabs_done, 1)
            for p in range(2):
                sp.sem_inc(stored[p], 16 * PER)
            with sp.Fori(0, STORE_ROUNDS) as i:
                cls = load_values(sp, cls_regs, cls_tab, i * RING + 2, EMPTY)
                for n in range(RING):
                    g = i * RING + n
                    p = (n + 2) % RING
                    with sp.If(cls[n] < EMPTY):
                        taken = load_values(sp, used, store_tab, (g + 2) * PER, B)
                        seqs = load_values(sp, idx, load_tab, (g + 2) * PER, B - 1)
                        sp.wait_ge(o_pool, upto(g))
                        sp.wait_ge(o_dve, upto(g))
                        sp.sem_inc(sp_turn, 1)
                        for j, s in enumerate(seqs):
                            sp.dma_start(out[bass.ds(s, 1), :, :].rearrange("a (q t) h -> (a q) t h", t=TT),
                                         o[p][j * ROWS:(j + 1) * ROWS, :, :], cond=(taken[j] > 0)
                                         ).then_inc(stored[p], 16)
                    with sp.Else():
                        sp.sem_inc(stored[p], 16 * PER)
            for p in range(RING):
                sp.wait_ge(stored[p], 16 * PER * (STORE_ROUNDS + (p < 2)))

        @block.gpsimd
        def _(pool):
            nc.gpsimd.memset(ident[:, :], 0.0).then_inc(pool_step, 1)
            nc.gpsimd.memset(tri[:, :, :], 1.0).then_inc(pool_step, 1)
            nc.gpsimd.memset(bias_rows[:, :], 0.0).then_inc(pool_step, 1)
            nc.gpsimd.iota(route_id[:, :], [[0, 1]], base=0, channel_multiplier=1,
                           allow_small_or_imprecise_dtypes=True).then_inc(consts, 1)
            nc.gpsimd.iota(full[:, :], [[PER, B // PER]], base=0, channel_multiplier=0,
                           allow_small_or_imprecise_dtypes=True).then_inc(consts, 1)
            nc.gpsimd.iota(step_id[:, :], [[1, CLS]], base=-2, channel_multiplier=0,
                           allow_small_or_imprecise_dtypes=True).then_inc(consts, 1)
            nc.gpsimd.iota(seq1[:, :], [[0, 1]], base=1, channel_multiplier=1,
                           allow_small_or_imprecise_dtypes=True).then_inc(consts, 1)
            nc.gpsimd.iota(place_id[:, :], [[1, PLACES]], base=-2 * PER, channel_multiplier=0,
                           allow_small_or_imprecise_dtypes=True).then_inc(consts, 1)
            nc.gpsimd.iota(first_place[:, :], [[PER, CLS + 1]], base=0, channel_multiplier=0,
                           allow_small_or_imprecise_dtypes=True).then_inc(consts, 1)
            nc.gpsimd.iota(row_place[:, :], [[1, PER], [0, ROWS]], base=0, channel_multiplier=0,
                           allow_small_or_imprecise_dtypes=True).then_inc(consts, 1)
            nc.gpsimd.iota(row_1[:, :], [[0, PER], [1, ROWS]], base=1, channel_multiplier=ROWS,
                           allow_small_or_imprecise_dtypes=True).then_inc(consts, 1)
            nc.gpsimd.iota(minus_row[:, :], [[0, 1]], base=0, channel_multiplier=-1,
                           allow_small_or_imprecise_dtypes=True).then_inc(consts, 1)
            pool.wait_ge(pool_step, 3)
            for e in range(2):
                nc.gpsimd.affine_select(out=tri[:, e, :], in_=tri[:, e, :], compare_op=ALU.is_ge, fill=0.0,
                                        base=e - 1, pattern=[[1, ROUTES]], channel_multiplier=-1
                                        ).then_inc(consts, 1)
            nc.gpsimd.affine_select(out=ident[:, :], in_=ident[:, :], compare_op=ALU.not_equal, fill=1.0,
                                    base=0, pattern=[[-1, P]], channel_multiplier=1).then_inc(consts, 1)
            nc.gpsimd.memset(half[:, :], -0.5).then_inc(pool_step, 1)
            nc.gpsimd.memset(bf_raw[:, NONE * H:(NONE + 1) * H], 0.0).then_inc(bf_in, 16)
            nc.gpsimd.memset(ones2[:, :].bitcast(F32), 1.0).then_inc(bf_in, 16)
            for w in (wf_hi, wf_lo):
                nc.gpsimd.memset(w[:, NONE * KT * H:(NONE + 1) * KT * H].bitcast(F32), 0.0).then_inc(wf_lo_done, 1)

            x_rows = x.rearrange("b (q t) h -> (b q) (t h)", t=TT)

            def gather(p, index):
                nc.gpsimd.indirect_dma_start(
                    out=x_in[p][:, :, :].rearrange("p t h -> p (t h)"), out_offset=None, in_=x_rows,
                    in_offset=bass.IndirectOffsetOnAxis(ap=index, axis=0)).then_inc(x_loaded[p], 16)

            def gamma_beta(g, p, lo, hi):
                tiles = o[p][:, lo:hi, :]
                pool.wait_ge(z_done, upto(g, TT, hi - 1))
                nc.gpsimd.tensor_tensor(tiles, tiles, spread(gamma_b, hi - lo), ALU.mult).then_inc(gam_pool, 1)
                pool.wait_ge(gam_pool, upto(g))
                nc.gpsimd.tensor_tensor(tiles, tiles, spread(beta_b, hi - lo), ALU.add).then_inc(o_pool, 1)

            pool.wait_ge(rows_done, 1)
            gather(0, row_idx[:, 0:1])
            gather(1, row_idx[:, 1:2])
            gather(2, row_idx[:, 2:3])
            for i, (raw, _, hi, lo) in enumerate(W_PARTS[DVE_PARTS:]):
                pool.wait_ge(w_hi_done, DVE_PARTS + i + 1)
                nc.gpsimd.tensor_tensor(lo.rearrange("p k n -> p (k n)"), raw.rearrange("p k n -> p (k n)"), hi.bitcast(F32).rearrange("p k n -> p (k n)"), ALU.subtract).then_inc(wf_lo_done, 1)
            pool.wait_ge(pool_step, 4)
            pool.wait_ge(bcast_in, 16 * 2)
            nc.gpsimd.tensor_scalar(gamma_b[:, :], gamma_b[:, :], float(H) ** 0.5, None, ALU.mult
                                    ).then_inc(gamma_done, 1)
            pool.wait_ge(gamma_done, 1)

            for done, per in ((gam_pool, 1), (o_pool, 1), (row_done, 1), (rstd_step, 1), (rstd_done, 1)):
                pool.sem_inc(done, AHEAD * per)
            cls_regs = register_set(pool, "pool_cls", WINDOW)
            pool.wait_ge(tabs_done, 1)
            with pool.Fori(0, ROUNDS) as i:
                cls = load_values(pool, cls_regs, cls_tab, i * RING, EMPTY)
                for p in range(RING):
                    g = i * RING + p
                    with pool.If(cls[5 + p] < EMPTY):
                        nxt = (p + 3) % RING
                        nc.gpsimd.tensor_copy(row_cur[:, nxt:nxt + 1], row_idx[:, bass.ds(g + 3, 1)]
                                              ).then_inc(row_done, 1)
                        pool.wait_ge(y_done, upto(g - 1, 2))
                        pool.wait_ge(row_done, upto(g))
                        pool.sem_inc(pool_turn, 1)
                        gather(nxt, row_cur[:, nxt:nxt + 1])
                    with pool.If(cls[1 + p] < EMPTY):
                        q = (p + 1) % 2
                        pool.wait_ge(mv_done, upto(g - 1))
                        nc.gpsimd.tensor_tensor(rstd[q][:, :], hvar[q][:, :], half[:, :], ALU.pow
                                                ).then_inc(rstd_step, 1)
                        pool.wait_ge(rstd_step, upto(g - 1))
                        nc.gpsimd.tensor_tensor(shift[q][:, :], rstd[q][:, :], neg_mean[q][:, :], ALU.mult
                                                ).then_inc(rstd_done, 1)
                    with pool.If(cls[p] < EMPTY):
                        with pool.If(cls[2 + p] < EMPTY):
                            gamma_beta(g - 2, p, 0, POOL_TT)
                        with pool.Else():
                            gamma_beta(g - 2, p, TT - 1, TT)

        @block.scalar
        def _(act):
            act.wait_ge(consts, CONSTS)
            act.wait_ge(pool_step, 3)
            for row, b in ((0, b1_sr), (4 * NR, b1_nr), (4 * TSR, b1_tsr), (14, b2_sr)):
                n = b.shape[0] // P
                act.dma_start(bias_rows[row:row + n, :], b.rearrange("(m p) -> m p", p=P)).then_inc(rows_in, 16)
            for r, b in ((SR, b3_sr), (NR, b2_nr), (TSR, b2_tsr)):
                act.dma_start(bf_raw[:, r * H:(r + 1) * H], b.rearrange("(a n) -> a n", a=1).broadcast_to([2, H])
                              ).then_inc(bf_in, 16)
            for dst, b in ((gamma_b, gamma), (beta_b, beta)):
                act.dma_start(dst[:, :], b.rearrange("(a n) -> a n", a=1).broadcast_to([P, H])
                              ).then_inc(bcast_in, 16)
            nc.scalar.activation(warm[:, :], ident[0:1, 0:1], ACT.Gelu)
            for i, (raw, _, hi, _) in enumerate(W_PARTS):
                act.wait_ge(w_in[i], 16)
                nc.scalar.activation(hi, raw, ACT.Copy).then_inc(w_hi_done, 1)
            for done, per in ((x_hi_done, KT), (a_gelu, 2), (b_gelu, 2), (c_gelu, 2), (z_done, TT)):
                act.sem_inc(done, AHEAD * per)
            act.wait_ge(bias_done, 1)

            def x_high(g, p):
                for kt in range(KT):
                    act.wait_ge(xT_ready, upto(g, KT, kt))
                    nc.scalar.activation(x_hi[p][:, kt, :], ps_x[kt][:, :], ACT.Copy).then_inc(x_hi_done, 1)

            x_high(0, 0)
            act.wait_ge(bf_in, 16 * 5)
            nc.scalar.activation(bf_round[:, :], bf_raw[:, :], ACT.Copy).then_inc(bf_rounded, 1)
            cls_regs = register_set(act, "act_cls", WINDOW)

            def gelu(src, full, hi, bias, done):
                nc.scalar.activation(full, src, ACT.Gelu, bias=bias)
                nc.scalar.activation(hi, src, ACT.Gelu, bias=bias).then_inc(done, 1)

            act.wait_ge(tabs_done, 1)
            with act.Fori(0, ROUNDS) as i:
                cls = load_values(act, cls_regs, cls_tab, i * RING, EMPTY)
                for p in range(RING):
                    g = i * RING + p
                    with act.If(cls[3 + p] < EMPTY):
                        x_high(g + 1, (p + 1) % 2)
                    with act.If(cls[2 + p] >= NR):
                        with act.If(cls[2 + p] < EMPTY):
                            bias_at = act.snap(cls[2 + p].with_bounds(max_val=NONE) * 4)
                            for m in range(2):
                                act.wait_ge(a_ready, upto(g, 2, m))
                                act.wait_ge(f_split, upto(g - 1, 2, m))
                                gelu(ps_a[m][:, :], a_act[:, m, :], f_hi[p % 2][:, m, :],
                                     bias_cols[:, bass.ds(bias_at + m, 1)], a_gelu)
                    with act.Else():
                        for m in range(2):
                            act.wait_ge(a_ready, upto(g, 2, m))
                            act.wait_ge(f_split, upto(g - 1, 2, m))
                            gelu(ps_a[m][:, :], a_act[:, m, :], h_hi[:, m, :], bias_cols[:, m:m + 1], a_gelu)
                        for m in range(2):
                            act.wait_ge(b_ready, upto(g, 2, m))
                            gelu(ps_b[m][:, :], b_act[:, m, :], h_hi[:, 2 + m, :],
                                 bias_cols[:, 2 + m:3 + m], b_gelu)
                    with act.If(cls[p] < EMPTY):
                        act.wait_ge(rstd_done, upto(g - 2))
                        act.wait_ge(stored[p], 16 * PER * i)
                        for t in range(TT):
                            nc.scalar.activation(o[p][:, t, :], y[p % 2][:, t, :], ACT.Identity,
                                                 bias=shift[p % 2][:, t:t + 1], scale=rstd[p % 2][:, t:t + 1]
                                                 ).then_inc(z_done, 1)
                    with act.If(cls[2 + p] < NR):
                        for m in range(2):
                            act.wait_ge(c_ready, upto(g, 2, m))
                            gelu(ps_b[m][:, :], c_act[:, m, :], f_hi[p % 2][:, m, :],
                                 bias_cols[:, 14 + m:15 + m], c_gelu)

        @block.vector
        def _(dve):
            step = [0]

            def chain(ins):
                step[0] += 1
                ins.then_inc(dve_step, 1)
                dve.wait_ge(dve_step, step[0])

            chain(nc.vector.memset(ones4[:, :], 1.0))
            chain(nc.vector.memset(zeros[:, :], 0.0))
            dve.wait_ge(cond_in, 16)
            chain(nc.vector.tensor_copy(cond_f[:, :], cond_b[:, :]))
            for j, (value, less) in enumerate(((2, NONE - SR), (0, NONE - NR), (1, NONE - TSR))):
                chain(nc.vector.tensor_scalar(key[:, j, :], cond_f[:, :], float(value), float(-less),
                                              ALU.is_equal, ALU.mult))
            chain(nc.vector.tensor_tensor(key[:, 0, :], key[:, 0, :], key[:, 1, :], ALU.add))
            chain(nc.vector.scalar_tensor_tensor(out=key[:, 1, :], in0=key[:, 0, :], scalar=float(NONE),
                                                 in1=key[:, 2, :], op0=ALU.add, op1=ALU.add))
            dve.wait_ge(consts, CONSTS)
            chain(nc.vector.tensor_scalar(onehot[:, :], key[:, 1, :], route_id[:, 0:1], None, ALU.is_equal))
            chain(nc.vector.tensor_tensor_scan(rank[:, :], onehot[:, :], zeros[:, :], 0.0, ALU.add, ALU.add))
            chain(nc.vector.tensor_scalar(over[:, :], full[:, :], rank[:, B - 1:B], None, ALU.is_lt))
            nc.vector.tensor_reduce(groups[:, :], over[:, :], AX.X, ALU.add).then_inc(groups_done, 1)
            dve.wait_ge(bounds_ps, 1)
            chain(nc.vector.tensor_copy(bounds[:, :], bounds_pt))
            chain(nc.vector.tensor_scalar(place_m[:, 0, :], rank[:, :], -1.0, None, ALU.add))
            chain(nc.vector.tensor_scalar(bounds[:, 0:1], bounds[:, 0:1], float(PER), None, ALU.mult))
            chain(nc.vector.tensor_scalar(place_m[:, 0, :], place_m[:, 0, :], bounds[:, 0:1], None, ALU.add))
            nc.vector.tensor_tensor(place_m[:, 1, :], place_m[:, 0, :], onehot[:, :], ALU.mult
                                    ).then_inc(place_done, 1)
            chain(nc.vector.tensor_scalar(ended[:, 0, :], step_id[:, :], bounds[:, 1:2], None, ALU.is_ge))
            chain(nc.vector.tensor_scalar(ended[:, 1, :], step_id[:, :], 0.0, None, ALU.is_lt))
            chain(nc.vector.tensor_tensor(ended[:, 0, :], ended[:, 0, :], ended[:, 1, :], ALU.add))
            dve.wait_ge(place_ps, 1)
            chain(nc.vector.tensor_copy(place_col[:, :], place_pt))
            chain(nc.vector.tensor_scalar(reached[:, :], first_place[:, :], place_col[:, 0:1], None, ALU.is_le))
            chain(nc.vector.tensor_tensor(in_group[:, :], reached[:, 0:CLS], reached[:, 1:CLS + 1], ALU.subtract))
            chain(nc.vector.tensor_reduce(nth_group[:, :], reached[:, 1:CLS + 1], AX.X, ALU.add))
            chain(nc.vector.scalar_tensor_tensor(out=in_place[:, :], in0=nth_group[:, :], scalar=-float(PER),
                                                 in1=place_col[:, :], op0=ALU.mult, op1=ALU.add))
            nc.vector.scalar_tensor_tensor(out=row_at[:, :], in0=row_place[:, :], scalar=in_place[:, 0:1],
                                           in1=row_1[:, :], op0=ALU.is_equal, op1=ALU.mult
                                           ).then_inc(onehot_done, 1)
            nc.vector.tensor_scalar(at_place[:, :], place_id[:, :], place_col[:, 0:1], None, ALU.is_equal
                                    ).then_inc(onehot_done, 1)
            dve.wait_ge(rows_ps, 1)
            chain(nc.vector.tensor_scalar(row_f[:, :], rows_pt, -1.0, 0.0, ALU.add, ALU.max))
            nc.vector.tensor_copy(row_idx[:, :], row_f[:, :]).then_inc(rows_done, 1)
            dve.wait_ge(tabs_ps, 1)
            nc.vector.tensor_copy(cls_tab[:, :], cls_pt)
            nc.vector.tensor_copy(store_tab[:, :], perm_pt)
            chain(nc.vector.tensor_scalar(load_f[:, :], perm_pt, -1.0, 0.0, ALU.add, ALU.max))
            nc.vector.tensor_copy(load_tab[:, :], load_f[:, :]).then_inc(tabs_done, 1)

            dve.wait_ge(rows_t, 1)
            nc.vector.tensor_copy(bias_cols[:, :], bias_pt).then_inc(bias_done, 1)
            for i, (raw, _, hi, lo) in enumerate(W_PARTS[:DVE_PARTS]):
                dve.wait_ge(w_hi_done, i + 1)
                nc.vector.tensor_tensor(lo, raw, hi.bitcast(F32), ALU.subtract).then_inc(w_lo_done, 1)
            for done, per in ((x_lo_done, KT), (a_split, 2), (b_split, 2), (f_split, 2), (gam_dve, 1), (o_dve, 1),
                              (y_done, 2), (bn_done, TT), (agg_step, 4), (mv_done, 1)):
                dve.sem_inc(done, AHEAD * per)

            def x_low(g, p):
                for kt in range(KT):
                    dve.wait_ge(x_hi_done, upto(g, KT, kt))
                    nc.vector.tensor_tensor(x_lo[p][:, kt, :], ps_x[kt][:, :], x_hi[p][:, kt, :].bitcast(F32),
                                            ALU.subtract).then_inc(x_lo_done, 1)

            def times_gamma(g, p, lo, hi):
                dve.wait_ge(z_done, upto(g, TT, hi - 1))
                nc.vector.tensor_tensor(o[p][:, lo:hi, :], o[p][:, lo:hi, :], spread(gamma_b, hi - lo), ALU.mult
                                        ).then_inc(gam_dve, 1)

            def plus_beta(g, p, lo, hi):
                dve.wait_ge(gam_dve, upto(g))
                nc.vector.tensor_tensor(o[p][:, lo:hi, :], o[p][:, lo:hi, :], spread(beta_b, hi - lo), ALU.add
                                        ).then_inc(o_dve, 1)

            x_low(0, 0)
            dve.wait_ge(bf_rounded, 1)
            nc.vector.scalar_tensor_tensor(out=bf_parts[:, :], in0=bf_round[:, :].bitcast(F32),
                                           scalar=minus_row[:, 0:1], in1=bf_raw[:, :], op0=ALU.mult, op1=ALU.add
                                           ).then_inc(bf_done, 1)
            dve.wait_ge(gamma_done, 1)
            def lows(done, at, srcs, hi, lo, split, g):
                for m in range(2):
                    dve.wait_ge(done, upto(g, 2, m))
                    nc.vector.tensor_tensor(lo[:, at + m, :], srcs[:, m, :], hi[:, at + m, :].bitcast(F32),
                                            ALU.subtract).then_inc(split, 1)

            def nothing():
                pass

            def y_and_moments(g, q, x_g, between=nothing, after=nothing):
                dve.wait_ge(z_done, upto(g - 2, TT))
                for b in range(2):
                    dve.wait_ge(f_ready, upto(g, 2, b))
                    nc.vector.tensor_tensor(
                        y[q][:, 2 * b:2 * b + 2, :], ps_f[b][:, :].rearrange("p (t h) -> p t h", t=2),
                        x_g[:, 2 * b:2 * b + 2, :], ALU.add).then_inc(y_done, 1)
                between()
                for t in range(TT):
                    dve.wait_ge(y_done, upto(g, 2, t // 2))
                    nc.vector.bn_stats(stats[:, t, :], y[q][:, t, :]).then_inc(bn_done, 1)
                mean_e, m2_e, mean_o, m2_o = (stats[:, :, c] for c in (1, 2, 4, 5))
                dve.wait_ge(bn_done, upto(g, TT))
                nc.vector.tensor_tensor(diff[:, :], mean_e, mean_o, ALU.subtract).then_inc(agg_step, 1)
                nc.vector.tensor_tensor(m2[:, :], m2_e, m2_o, ALU.add).then_inc(agg_step, 1)
                nc.vector.tensor_scalar(mean_h[:, :], mean_e, -0.5, None, ALU.mult).then_inc(agg_step, 1)
                dve.wait_ge(agg_step, upto(g, 4, 0))
                nc.vector.scalar_tensor_tensor(out=diff2[:, :], in0=diff[:, :], scalar=H / 4.0,
                                               in1=diff[:, :], op0=ALU.mult, op1=ALU.mult).then_inc(agg_step, 1)
                dve.wait_ge(agg_step, upto(g, 4, 2))
                nc.vector.scalar_tensor_tensor(out=neg_mean[q][:, :], in0=mean_o, scalar=-0.5,
                                               in1=mean_h[:, :], op0=ALU.mult, op1=ALU.add)
                dve.wait_ge(agg_step, upto(g, 4, 3))
                nc.vector.scalar_tensor_tensor(out=hvar[q][:, :], in0=m2[:, :], scalar=H * EPS,
                                               in1=diff2[:, :], op0=ALU.add, op1=ALU.add).then_inc(mv_done, 1)
                after()

            def earlier_groups(cls, g, p):
                y_of = (g - 1, (p + 1) % 2, x_in[(p - 1) % RING])
                last = (g - 2, p, POOL_TT, TT)
                with dve.If(cls[p] < EMPTY):
                    y_and_moments(*y_of, between=lambda: times_gamma(*last), after=lambda: plus_beta(*last))
                with dve.Else():
                    with dve.If(cls[1 + p] < EMPTY):
                        y_and_moments(*y_of)

            def next_x(cls, g, p):
                with dve.If(cls[3 + p] < EMPTY):
                    x_low(g + 1, (p + 1) % 2)

            cls_regs = register_set(dve, "dve_cls", WINDOW)
            with dve.Fori(0, ROUNDS) as i:
                cls = load_values(dve, cls_regs, cls_tab, i * RING, EMPTY)
                for p in range(RING):
                    g = i * RING + p
                    f_now = (f_hi[p % 2], f_lo[p % 2], f_split, g)
                    with dve.If(cls[2 + p] >= NR):
                        with dve.If(cls[2 + p] < EMPTY):
                            next_x(cls, g, p)
                            lows(a_gelu, 0, a_act, *f_now)
                            earlier_groups(cls, g, p)
                        with dve.Else():
                            with dve.If(cls[1 + p] < EMPTY):
                                y_and_moments(g - 1, (p + 1) % 2, x_in[(p - 1) % RING])
                            with dve.If(cls[p] < EMPTY):
                                times_gamma(g - 2, p, 0, TT - 1)
                                plus_beta(g - 2, p, 0, TT - 1)
                    with dve.Else():
                        next_x(cls, g, p)
                        lows(a_gelu, 0, a_act, h_hi, h_lo, a_split, g)
                        lows(b_gelu, 2, b_act, h_hi, h_lo, b_split, g)
                        earlier_groups(cls, g, p)
                        lows(c_gelu, 0, c_act, *f_now)

        @block.tensor
        def _(pe):
            pe.wait_ge(consts, CONSTS)
            pe.wait_ge(groups_done, 1)
            for e in range(2):
                mm = nc.tensor.matmul(bounds_pt[:, e:e + 1], tri[:, e, :], groups[:, :], start=True, stop=True)
            mm.then_inc(bounds_ps, 1)
            pe.wait_ge(place_done, 1)
            nc.tensor.matmul(place_pt, place_m[:, 1, :], ones4[:, :], start=True, stop=True).then_inc(place_ps, 1)
            pe.wait_ge(onehot_done, 1)
            nc.tensor.matmul(rows_pt, row_at[:, :], in_group[:, :], start=True, stop=True).then_inc(rows_ps, 1)
            pe.wait_ge(onehot_done, 2)
            nc.tensor.matmul(perm_pt, seq1[:, :], at_place[:, :], start=True, stop=True)
            nc.tensor.matmul(cls_pt, ones4[:, :], ended[:, 0, :], start=True, stop=True).then_inc(tabs_ps, 1)
            pe.wait_ge(rows_in, 16 * 4)
            nc.tensor.transpose(bias_pt, bias_rows[:, :], ident[0:16, 0:16]).then_inc(rows_t, 1)

            def transpose_x(g, p, nth):
                pe.wait_ge(x_loaded[p], 16 * nth)
                for kt in range(KT):
                    for t in range(TT):
                        mm = nc.tensor.transpose(ps_x[kt][:, t * P:(t + 1) * P],
                                                 x_in[p][:, t, kt * P:(kt + 1) * P], ident[:, :])
                    mm.then_inc(xT_ready, 1)

            def layer1(route, m, p, dst):
                cols = slice(L1_COL[route] + m * P, L1_COL[route] + (m + 1) * P)
                for kt in range(KT):
                    nc.tensor.matmul(dst, w1_lo[:, kt, cols], x_hi[p % 2][:, kt, :], start=(kt == 0), stop=False)
                    nc.tensor.matmul(dst, w1_hi[:, kt, cols], x_lo[p % 2][:, kt, :], start=False, stop=False)
                    mm = nc.tensor.matmul(dst, w1_hi[:, kt, cols], x_hi[p % 2][:, kt, :], start=False,
                                          stop=(kt == KT - 1))
                return mm

            def layer1_a(route, g, p):
                pe.wait_ge(w_lo_done, route + 1)
                for m in range(2):
                    pe.wait_ge(a_gelu, upto(g - 1, 2, m))
                    layer1(route, m, p, ps_a[m][:, :]).then_inc(a_ready, 1)

            for done, per in ((xT_ready, KT), (a_ready, 2), (b_ready, 2), (c_ready, 2), (f_ready, 2)):
                pe.sem_inc(done, AHEAD * per)
            pe.wait_ge(bias_done, 1)
            pe.wait_ge(tabs_done, 1)
            transpose_x(0, 0, 1)
            cls_regs = register_set(pe, "pe_cls", WINDOW)
            with pe.Fori(0, ROUNDS) as i:
                cls = load_values(pe, cls_regs, cls_tab, i * RING, EMPTY)
                for p in range(RING):
                    g = i * RING + p
                    with pe.If(cls[2 + p] < EMPTY):
                        pe.wait_ge(x_lo_done, upto(g, KT))
                        with pe.If(cls[3 + p] < EMPTY):
                            transpose_x(g + 1, (p + 1) % RING, i + 1 + (p + 1) // RING)
                        with pe.If(cls[2 + p] < NR):
                            layer1_a(SR, g, p)
                            for m in range(2):
                                if m == 0:
                                    pe.wait_ge(c_gelu, upto(g - 1, 2))
                                layer1(SR, 2 + m, p, ps_b[m][:, :]).then_inc(b_ready, 1)
                        with pe.Else():
                            with pe.If(cls[2 + p] < TSR):
                                layer1_a(NR, g, p)
                            with pe.Else():
                                layer1_a(TSR, g, p)
                    with pe.If(cls[1 + p] < EMPTY):
                        q = (p + 1) % 2
                        pe.wait_ge(wf_lo_done, 2 + len(W_PARTS) - DVE_PARTS)
                        pe.wait_ge(bf_done, 1)
                        pe.wait_ge(f_split, upto(g - 1, 2))
                        f_at = pe.snap(cls[1 + p].with_bounds(max_val=NONE) * (KT * H))
                        b_at = pe.snap(cls[1 + p].with_bounds(max_val=NONE) * H)
                        for t in range(TT):
                            dst = ps_f[t // 2][:, (t % 2) * H:(t % 2 + 1) * H]
                            if t % 2 == 0:
                                pe.wait_ge(y_done, upto(g - 2, 2, t // 2))
                            for kt in range(KT):
                                toks = slice(t * P, (t + 1) * P)
                                w_hi = wf_hi[:, bass.ds(f_at + kt * H, H)]
                                w_lo = wf_lo[:, bass.ds(f_at + kt * H, H)]
                                nc.tensor.matmul(dst, f_lo[q][:, kt, toks], w_hi, start=(kt == 0), stop=False)
                                nc.tensor.matmul(dst, f_hi[q][:, kt, toks], w_lo, start=False, stop=False)
                                nc.tensor.matmul(dst, f_hi[q][:, kt, toks], w_hi, start=False, stop=False)
                            mm = nc.tensor.matmul(dst, ones2[:, :], bf_parts[:, bass.ds(b_at, H)],
                                                  start=False, stop=True)
                            if t % 2:
                                mm.then_inc(f_ready, 1)
                    with pe.If(cls[2 + p] < NR):
                        for m in range(2):
                            dst = ps_b[m][:, :]
                            cols = slice(m * P, (m + 1) * P)
                            pe.wait_ge(b_gelu, upto(g, 2, m))
                            for kt in range(HT):
                                if m == 0 and kt == 0:
                                    pe.wait_ge(w_lo_done, DVE_PARTS)
                                    pe.wait_ge(a_split, upto(g, 2))
                                if m == 0 and kt >= 2:
                                    pe.wait_ge(b_split, upto(g, 2, kt - 2))
                                nc.tensor.matmul(dst, w2_lo[:, kt, cols], h_hi[:, kt, :], start=(kt == 0),
                                                 stop=False)
                                nc.tensor.matmul(dst, w2_hi[:, kt, cols], h_lo[:, kt, :], start=False,
                                                 stop=False)
                                mm = nc.tensor.matmul(dst, w2_hi[:, kt, cols], h_hi[:, kt, :], start=False,
                                                      stop=(kt == HT - 1))
                            mm.then_inc(c_ready, 1)


INPUTS = ["x", "itok_B_0_2"] + ["L0_cond_" + n for n in (
    "w1_nr", "b1_nr", "w2_nr", "b2_nr", "w1_tsr", "b1_tsr", "w2_tsr", "b2_tsr",
    "w1_sr", "b1_sr", "w2_sr", "b2_sr", "w3_sr", "b3_sr", "gamma", "beta")]


def kernel(**inputs):
    import numpy as np
    import concourse.bacc as bacc
    from concourse.bass_utils import run_bass_kernel_spmd

    nc = bacc.Bacc("TRN2", target_bir_lowering=False, num_devices=1)
    arrays, args = {}, []
    for name in INPUTS:
        a = np.ascontiguousarray(inputs[name])
        arrays[f"{name}_dram"] = a
        args.append(nc.dram_tensor(f"{name}_dram", a.shape, mybir.dt.from_np(a.dtype), kind="ExternalInput").ap())
    args.append(nc.dram_tensor("out_dram", inputs["x"].shape, F32, kind="ExternalOutput").ap())
    build_cond_mlp(nc, *args)
    result = run_bass_kernel_spmd(nc, [arrays], core_ids=[0])
    return result.results[0]["out_dram"]
```
